# Optimizing a Trainium2 kernel written in Bass

```python
import numpy as np
import jax
import jax.numpy as jnp

def _softmax(x, axis=-1):
    return jax.nn.softmax(x, axis=axis)

def _gelu(x):
    return jax.nn.gelu(x, approximate=True)

def _silu(x):
    return jax.nn.silu(x)

def _sigmoid(x):
    return jax.nn.sigmoid(x)

def _layernorm(x, axis=-1, eps=1e-05):
    m = jnp.mean(x, axis=axis, keepdims=True)
    v = jnp.var(x, axis=axis, keepdims=True)
    return (x - m) / jnp.sqrt(v + eps)

def _scatter_add(tgt, idx, src, axis=0):
    return tgt.at[idx].add(src)

def _segment_sum(src, seg, n):
    return jax.ops.segment_sum(src, seg, n)
kernel_name = 'mk_flamingo_gated_d1_seqx_r8_ede1b4'

def setup_inputs(seed: int=0):
    np.random.seed(seed)
    _w = jnp.asarray

    def _rec_inputs():
        import jax
        import jax.numpy as jnp
        _rk = jax.random.key(seed)
        x = -0.0002928 + 1 * jax.random.normal(jax.random.fold_in(_rk, 1), (8, 256, 128), jnp.float32)
        _lenS = 256 - jax.random.randint(jax.random.fold_in(_rk, 7), (8,), 0, max(1, 256 // 4) + 1, jnp.int32)
        _lenS2 = 256 - jax.random.randint(jax.random.fold_in(_rk, 8), (8,), 0, max(1, 256 // 4) + 1, jnp.int32)
        _ctx_1024P = jax.random.normal(jax.random.fold_in(_rk, 11), (8, 16, 128), jnp.float32)
        _ctx_1024c = jax.random.dirichlet(jax.random.fold_in(_rk, 511), 0.3 * jnp.ones((16,), jnp.float32), (8, 256))
        _ctx_1024t = jnp.einsum('bsk,bkd->bsd', _ctx_1024c, _ctx_1024P)
        _ctx_1024t = _ctx_1024t * jax.lax.rsqrt(jnp.mean(jnp.square(_ctx_1024t)) + 1e-12) * 0.953939
        ctx_1024 = -1.39393e-06 + 0.999914 * (_ctx_1024t + 0.3 * jax.random.normal(jax.random.fold_in(_rk, 611), (8, 256, 128), jnp.float32))
        _g = jax.random.normal(jax.random.fold_in(_rk, 9001), (2, 1), jnp.float32)
        _g = jnp.sign(_g) * jnp.maximum(jnp.abs(_g), 1.0) + (_g == 0) * 1.0
        g_xattn = _g[0]
        g_ffn = _g[1]
        return (x, ctx_1024, g_xattn, g_ffn)
    x, ctx_1024, g_xattn, g_ffn = _rec_inputs()

    def _L0_xattn_setup():
        import jax, jax.numpy as jnp
        import numpy as np
        N_HEAD = 16
        MAX_SEQ_LEN = 256
        RATIO = 1
        NEG_INF = -jnp.inf

        def make_alibi_bias(n_head: int, max_seq_len: int, ratio: int) -> jnp.ndarray:
            s = jnp.arange(max_seq_len)[None, :] * ratio
            t = jnp.arange(max_seq_len * ratio)[:, None]
            bias = (s - t).astype(jnp.float32)
            bias = jnp.where(bias > 0, NEG_INF, bias)
            m = jnp.cumprod(jnp.full((n_head,), 2.0 ** (-8.0 / n_head), dtype=jnp.float32))
            return bias[None, :, :] * m[:, None, None]
        key = jax.random.key(seed)
        kq, kk, kv = jax.random.split(key, 3)
        B, T, D = (2, 256, 128)
        return {'q': jax.random.normal(kq, (B, T, D), dtype=jnp.float32), 'k': jax.random.normal(kk, (B, T, D), dtype=jnp.float32), 'v': jax.random.normal(kv, (B, T, D), dtype=jnp.float32)}
    _L0_xattn_all = _L0_xattn_setup()
    _L0_xattn_in = {k: v for k, v in _L0_xattn_all.items() if k in ()}
    del _L0_xattn_all

    def _L0_ffn_setup():
        import jax, jax.numpy as jnp
        import numpy as np
        DIM = 128
        E = 16
        TOPK = 2
        G = 4
        TOPK_G = 2
        INTER = 64
        N_SHARED = 2
        ROUTE_SCALE = 1.0

        def _gate(xf, gate_w, gate_b):
            scores = xf @ gate_w.T
            scores = jax.nn.softmax(scores.astype(jnp.float32), axis=-1)
            orig = scores
            scores = scores + gate_b
            T = xf.shape[0]
            sg = scores.reshape(T, G, E // G)
            group_scores = jax.lax.top_k(sg, 2)[0].sum(-1)
            _, gidx = jax.lax.top_k(group_scores, TOPK_G)
            keep = jax.nn.one_hot(gidx, G).sum(axis=1) > 0
            sg = jnp.where(keep[:, :, None], sg, -jnp.inf)
            scores = sg.reshape(T, E)
            _, idx = jax.lax.top_k(scores, TOPK)
            weights = jnp.take_along_axis(orig, idx, axis=1)
            weights = (weights * ROUTE_SCALE).astype(xf.dtype)
            return (weights, idx)
        key = jax.random.key(seed)
        ks = jax.random.split(key, 16)
        s = lambda fan_in: 1.0 / np.sqrt(fan_in)
        inp = {'x': jax.random.normal(ks[0], (4, 128, DIM), dtype=jnp.float32), 'gate_w': jax.random.normal(ks[1], (E, DIM), dtype=jnp.float32) * s(DIM), 'gate_b': jnp.zeros((E,), dtype=jnp.float32), 'We1': jax.random.normal(ks[2], (E, DIM, INTER), dtype=jnp.float32) * s(DIM), 'be1': jnp.zeros((E, INTER), dtype=jnp.float32), 'We2': jax.random.normal(ks[3], (E, INTER, DIM), dtype=jnp.float32) * s(INTER), 'be2': jnp.zeros((E, DIM), dtype=jnp.float32), 'We3': jax.random.normal(ks[4], (E, DIM, INTER), dtype=jnp.float32) * s(DIM), 'be3': jnp.zeros((E, INTER), dtype=jnp.float32), 'ws1': jax.random.normal(ks[5], (DIM, N_SHARED * INTER), dtype=jnp.float32) * s(DIM), 'bs1': jnp.zeros((N_SHARED * INTER,), dtype=jnp.float32), 'ws2': jax.random.normal(ks[6], (N_SHARED * INTER, DIM), dtype=jnp.float32) * s(N_SHARED * INTER), 'bs2': jnp.zeros((DIM,), dtype=jnp.float32), 'ws3': jax.random.normal(ks[7], (DIM, N_SHARED * INTER), dtype=jnp.float32) * s(DIM), 'bs3': jnp.zeros((N_SHARED * INTER,), dtype=jnp.float32)}
        return inp
    _L0_ffn_all = _L0_ffn_setup()
    _L0_ffn_in = {k: v for k, v in _L0_ffn_all.items() if k in ('gate_w', 'gate_b', 'We1', 'be1', 'We2', 'be2', 'We3', 'be3', 'ws1', 'bs1', 'ws2', 'bs2', 'ws3', 'bs3')}
    del _L0_ffn_all
    return {'x': x, 'ctx_1024': ctx_1024, 'g_xattn': g_xattn, 'g_ffn': g_ffn, 'L0_ffn_gate_w': _L0_ffn_in['gate_w'], 'L0_ffn_gate_b': _L0_ffn_in['gate_b'], 'L0_ffn_We1': _L0_ffn_in['We1'], 'L0_ffn_be1': _L0_ffn_in['be1'], 'L0_ffn_We2': _L0_ffn_in['We2'], 'L0_ffn_be2': _L0_ffn_in['be2'], 'L0_ffn_We3': _L0_ffn_in['We3'], 'L0_ffn_be3': _L0_ffn_in['be3'], 'L0_ffn_ws1': _L0_ffn_in['ws1'], 'L0_ffn_bs1': _L0_ffn_in['bs1'], 'L0_ffn_ws2': _L0_ffn_in['ws2'], 'L0_ffn_bs2': _L0_ffn_in['bs2'], 'L0_ffn_ws3': _L0_ffn_in['ws3'], 'L0_ffn_bs3': _L0_ffn_in['bs3']}

def reference(x, ctx_1024, g_xattn, g_ffn, L0_ffn_gate_w, L0_ffn_gate_b, L0_ffn_We1, L0_ffn_be1, L0_ffn_We2, L0_ffn_be2, L0_ffn_We3, L0_ffn_be3, L0_ffn_ws1, L0_ffn_bs1, L0_ffn_ws2, L0_ffn_bs2, L0_ffn_ws3, L0_ffn_bs3):
    import jax
    import jax.numpy as jnp

    def _L0_xattn_ref(q, k, v):
        import jax, jax.numpy as jnp
        import numpy as np
        N_HEAD = 16
        MAX_SEQ_LEN = 256
        RATIO = 1
        NEG_INF = -jnp.inf

        def make_alibi_bias(n_head: int, max_seq_len: int, ratio: int) -> jnp.ndarray:
            s = jnp.arange(max_seq_len)[None, :] * ratio
            t = jnp.arange(max_seq_len * ratio)[:, None]
            bias = (s - t).astype(jnp.float32)
            bias = jnp.where(bias > 0, NEG_INF, bias)
            m = jnp.cumprod(jnp.full((n_head,), 2.0 ** (-8.0 / n_head), dtype=jnp.float32))
            return bias[None, :, :] * m[:, None, None]
        B, T, D = q.shape
        S = k.shape[1]
        H = N_HEAD
        dh = D // H
        qh = q.reshape(B, T, H, dh).transpose(0, 2, 1, 3)
        kh = k.reshape(B, S, H, dh).transpose(0, 2, 1, 3)
        vh = v.reshape(B, S, H, dh).transpose(0, 2, 1, 3)
        scores = jnp.einsum('bhtd,bhsd->bhts', qh, kh) / jnp.sqrt(jnp.float32(dh))
        bias = make_alibi_bias(H, MAX_SEQ_LEN, RATIO)[:, -T:, -S:]
        attn = jax.nn.softmax(scores + bias[None], axis=-1)
        out = jnp.einsum('bhts,bhsd->bhtd', attn, vh)
        return out.transpose(0, 2, 1, 3).reshape(B, T, D)

    def _L0_ffn_ref(x, gate_w, gate_b, We1, be1, We2, be2, We3, be3, ws1, bs1, ws2, bs2, ws3, bs3):
        import jax, jax.numpy as jnp
        import numpy as np
        DIM = 128
        E = 16
        TOPK = 2
        G = 4
        TOPK_G = 2
        INTER = 64
        N_SHARED = 2
        ROUTE_SCALE = 1.0

        def _gate(xf, gate_w, gate_b):
            scores = xf @ gate_w.T
            scores = jax.nn.softmax(scores.astype(jnp.float32), axis=-1)
            orig = scores
            scores = scores + gate_b
            T = xf.shape[0]
            sg = scores.reshape(T, G, E // G)
            group_scores = jax.lax.top_k(sg, 2)[0].sum(-1)
            _, gidx = jax.lax.top_k(group_scores, TOPK_G)
            keep = jax.nn.one_hot(gidx, G).sum(axis=1) > 0
            sg = jnp.where(keep[:, :, None], sg, -jnp.inf)
            scores = sg.reshape(T, E)
            _, idx = jax.lax.top_k(scores, TOPK)
            weights = jnp.take_along_axis(orig, idx, axis=1)
            weights = (weights * ROUTE_SCALE).astype(xf.dtype)
            return (weights, idx)
        shape = x.shape
        xf = x.reshape(-1, DIM)
        weights, idx = _gate(xf, gate_w, gate_b)
        combine = (jax.nn.one_hot(idx, E, dtype=xf.dtype) * weights[..., None]).sum(1)
        h1 = jnp.einsum('td,edi->tei', xf, We1) + be1
        h3 = jnp.einsum('td,edi->tei', xf, We3) + be3
        h = jax.nn.silu(h1) * h3
        yo = jnp.einsum('tei,eid->ted', h, We2) + be2
        y = jnp.einsum('te,ted->td', combine, yo)
        z = jax.nn.silu(xf @ ws1 + bs1) * (xf @ ws3 + bs3) @ ws2 + bs2
        return (y + z).reshape(shape)
    x = x + jnp.tanh(g_xattn[0]) * _L0_xattn_ref(_layernorm(x, axis=-1), ctx_1024, ctx_1024)
    x = x + jnp.tanh(g_ffn[0]) * _L0_ffn_ref(_layernorm(x, axis=-1), L0_ffn_gate_w, L0_ffn_gate_b, L0_ffn_We1, L0_ffn_be1, L0_ffn_We2, L0_ffn_be2, L0_ffn_We3, L0_ffn_be3, L0_ffn_ws1, L0_ffn_bs1, L0_ffn_ws2, L0_ffn_bs2, L0_ffn_ws3, L0_ffn_bs3)
    return x

_drawn_inputs = setup_inputs


def setup_inputs(seed=0):
    import zlib

    import numpy as np

    out = dict(_drawn_inputs(seed))
    spreads = {'L0_ffn_gate_b': (0.0, 0.1),
     'L0_ffn_be1': (0.0, 0.684),
     'L0_ffn_be2': (0.0, 0.43),
     'L0_ffn_be3': (0.0, 0.675),
     'L0_ffn_bs1': (0.0, 0.1),
     'L0_ffn_bs2': (0.0, 0.1),
     'L0_ffn_bs3': (0.0, 0.1)}
    factors = {}
    for name, (base, spread) in spreads.items():
        noise = np.random.default_rng([zlib.crc32(name.encode()), seed]).standard_normal(out[name].shape)
        drawn = base * np.exp(spread * noise) if base else spread * noise
        out[name] = jnp.asarray(drawn.astype(out[name].dtype))
    for name, factor in factors.items():
        out[name] = (out[name] * factor).astype(out[name].dtype)
    return out
```

```python
from contextlib import ExitStack
from itertools import count

import numpy as np

import concourse.bass as bass
from concourse import mybir

F32 = mybir.dt.float32
F32R = mybir.dt.float32r
BF16 = mybir.dt.bfloat16
ALU = mybir.AluOpType
ACT = mybir.ActivationFunctionType
AX_X = mybir.AxisListType.X

P = 128
B, SEQ, D = 8, 256, 128
TPB = SEQ // P
TILES = B * TPB
H = 16
DH = D // H
UPB = 4
HPU = H // UPB
HALVES = 2
HPH = H // HALVES
QUAD = 32
BANK = 512
UNITS = B * UPB
EPS = 1e-5
MASKED = -1e30

ROWS = 64
QK = 6 * DH
R_SLOPE = QK
R_MAX = QK + 3
K_S = QK + 3
K_ST = QK + 5

E, GROUPS, TOPK = 16, 4, 2
INTER = 64
EPC = P // INTER
RCH = E // EPC
CH = RCH + 1
KEEP_GROUPS = 2
GT = 4
NG = TILES // GT
SLOTS = 3
NB1 = 2 * CH + 1

C_ID, C_MASK, C_SLOPE, C_POS, C_E, C_LOWER = 0, P, 2 * P, 2 * P + 3 * H, 2 * P + 3 * H + TPB, 2 * P + 3 * H + TPB + E
C_END = C_LOWER + GROUPS * GROUPS


def to_bfloat16(v):
    bits = v.view(np.uint32)
    return ((bits + 0x7FFF + ((bits >> 16) & 1)) & np.uint32(0xFFFF0000)).view(np.float32)


def constants():
    c = np.zeros((P, C_END), np.float32)
    c[:, C_ID:C_ID + P] = np.eye(P)
    t, s = np.arange(P)[:, None], np.arange(P)[None, :]
    c[:, C_MASK:C_MASK + P] = np.where(s > t, MASKED, 0.0)
    rest = np.cumprod(np.full((H,), 2.0 ** (-8.0 / H), np.float32), dtype=np.float32)
    for part in range(3):
        piece = to_bfloat16(rest)
        c[:, C_SLOPE + part:C_SLOPE + 3 * H:3] = piece
        rest = rest - piece
    for n in range(TPB):
        c[:, C_POS + n] = np.arange(P) + n * P
    c[:, C_E:C_E + E] = E - np.arange(E)
    c[:, C_LOWER:C_END] = np.tril(np.ones((GROUPS, GROUPS)), -1).reshape(-1)
    spread = np.zeros((2 * E, RCH, P), np.float32)
    for e in range(E):
        spread[e, e // EPC, (e % EPC) * INTER:(e % EPC + 1) * INTER] = 1.0
        spread[E + e] = spread[e]
    return c, spread.reshape(2 * E, RCH * P)


def program(nc, x, ctx_in, g_xattn, g_ffn, gate_w, gate_b, We1, be1, We2, be2, We3, be3,
            ws1, bs1, ws2, bs2, ws3, bs3, const_in, spread_in, out):
    ctx = ExitStack()
    with ctx:
        def sb(name, shape, dt=F32):
            return ctx.enter_context(nc.sbuf_tensor(name, shape, dt))

        def sem(name):
            return ctx.enter_context(nc.semaphore(name))

        cst = sb("cst", [P, C_END])
        ident = cst[:, C_ID:C_ID + P]
        identb = sb("identb", [P, P], BF16)
        maskb = sb("maskb", [P, P], BF16)
        xs = sb("xs", [P, TILES, D])
        cs = sb("cs", [P, TILES, D])
        stats = sb("stats", [P, TPB, 6])
        mv = sb("mv", [P, TPB, 2])
        var8 = sb("var8", [P, TPB])
        minus_half = sb("minus_half", [P, TILES])
        rstd = sb("rstd", [P, TPB])
        qhat = sb("qhat", [P, HALVES, TPB, D // HALVES])
        kin = sb("kin", [P, HALVES, TPB, D // HALVES])
        qrest = sb("qrest", [P, TPB * HPH, DH])
        krest = sb("krest", [P, TPB * HPH, DH])
        qcat = sb("qcat", [P, HALVES, TPB, HPH, ROWS], BF16)
        kcat = sb("kcat", [P, HALVES, TPB, HPH, ROWS], BF16)
        vcat = sb("vcat", [P, HALVES, TPB, HPH, QUAD])
        qkT = sb("qkT", [P, UPB, 2, 2 * SEQ], BF16)
        q2T = sb("q2T", [P, 2, SEQ], BF16)
        negmax = sb("negmax", [P, 2, TPB, HPU])
        prob = sb("prob", [P, 2, HPU, 3 * P])
        avT = sb("avT", [P, 2, SEQ])
        rsum = sb("rsum", [P, TPB, HPU])
        onorm = sb("onorm", [P, TPB, HPU * DH])
        gl = sb("gl", [1, 2 + E])
        ones = sb("ones", [1, P])
        tg = sb("tg", [P, 2])
        gateb = sb("gateb", [P, E])
        gwr = sb("gwr", [E, D])
        gwT = sb("gwT", [P, 2, E], F32R)
        brow = sb("brow", [NB1, P])
        bcol = sb("bcol", [P, NB1])
        w13 = sb("w13", [P, 2, CH, P])
        w13h = sb("w13h", [P, 2, CH, P], F32R)
        w13l = sb("w13l", [P, 2, CH, P], F32R)
        w2 = sb("w2", [P, CH, D])
        be2f = sb("be2f", [3 * E, D])
        be2r = sb("be2r", [3 * E, D], F32R)
        spreadf = sb("spreadf", [2 * E, RCH * P])
        spreadr = sb("spreadr", [2 * E, RCH * P], F32R)
        stats2 = sb("stats2", [P, TILES, 6])
        mv2 = sb("mv2", [P, TILES, 2])
        var2 = sb("var2", [P, TILES])
        rstd2 = sb("rstd2", [P, TILES])
        xh = sb("xh", [P, 2, GT, D])
        xTh = sb("xTh", [P, B * SEQ], F32R)
        xTl = sb("xTl", [P, B * SEQ], F32R)
        wide = sb("wide", [P, 9, TILES, E])
        narrow = sb("narrow", [P, 8, TILES, GROUPS])
        minmax = sb("minmax", [P, 2, TILES * GROUPS, 2])
        rank = sb("rank", [P, 3, TILES, GROUPS, GROUPS])
        one = sb("one", [P, 7, TILES])
        c_hi = sb("c_hi", [P, TILES, E], F32R)
        ccat = sb("ccat", [P, TILES, 3, E])
        cT = sb("cT", [3 * E, B * SEQ], F32R)
        s1 = sb("s1", [P, SLOTS, SEQ])
        spreadc = sb("spreadc", [P, SLOTS, SEQ])
        u = sb("u", [P, SLOTS, SEQ])
        hid = sb("hid", [P, SLOTS, SEQ])
        yT = sb("yT", [P, SEQ])
        outb = sb("outb", [P, TPB, D])

        def psum(name, banks=1):
            return ctx.enter_context(nc.psum_tensor(name, [P, banks, BANK], F32))

        bank_t, bank_t2, bank_s, bank_st, bank_av, bank_ot = (
            psum("bank_t"), psum("bank_t2"), psum("bank_s", 2), psum("bank_st", 2), psum("bank_av"), psum("bank_ot"))
        ps_t = bank_t[:, 0, :].bitcast(BF16).rearrange("p (a n) -> p a n", a=2)
        ps_t2 = bank_t2[:, 0, 0:SEQ].bitcast(BF16).rearrange("p (a n) -> p a n", a=2)
        ps_xt = [bank_t[:, 0, :], bank_t2[:, 0, :]]
        ps_logit = bank_s[:, 0, 0:TILES * E].rearrange("p (n e) -> p n e", e=E)
        ps_w = bank_s[:, 1, :]
        ps_ct = [bank_av[0:3 * E, 0, :], bank_ot[0:3 * E, 0, :]]
        ps_h = [bank_t[:, 0, :], bank_t2[:, 0, :], bank_s[:, 0, :]]
        ps_c = [bank_s[:, 1, :], bank_st[:, 0, :], bank_st[:, 1, :]]
        ps_y, ps_yt = bank_av[:, 0, 0:SEQ], bank_ot[:, 0, 0:SEQ]

        x0_in, xr_in, c0_in, cr_in, cst_in, gl_in = (
            sem(n) for n in ("x0_in", "xr_in", "c0_in", "cr_in", "cst_in", "gl_in"))
        small_in, w13_in, w2_in = sem("small_in"), sem("w13_in"), sem("w2_in")
        ones_set = sem("ones_set")
        half_set = sem("half_set")
        rows_set = sem("rows_set")
        consts_set = sem("consts_set")
        gl_done = sem("gl_done")
        tg_ready = sem("tg_ready")
        stat_done = sem("stat_done")
        aggr_done = sem("aggr_done")
        var_ready = sem("var_ready")
        rstd_ready = sem("rstd_ready")
        kin_ready = sem("kin_ready")
        qhat_ready = sem("qhat_ready")
        q_step, k_step = sem("q_step"), sem("k_step")
        pool_passed, dve_passed = sem("pool_passed"), sem("dve_passed")
        q_built, k_built = sem("q_built"), sem("k_built")
        t_done = sem("t_done")
        qk_ready = sem("qk_ready")
        s_done = sem("s_done")
        max_done = sem("max_done")
        chi_done = sem("chi_done")
        c_ready = sem("c_ready")
        t2_done = sem("t2_done")
        q2_ready = sem("q2_ready")
        st_done = sem("st_done")
        exp_done = sem("exp_done")
        v_ready = sem("v_ready")
        av_done = sem("av_done")
        av_out = sem("av_out")
        ot_done = sem("ot_done")
        recip_done = sem("recip_done")
        o_read = sem("o_read")
        x1_ready = sem("x1_ready")
        stat2_done, aggr2_done, var2_ready = sem("stat2_done"), sem("aggr2_done"), sem("var2_ready")
        rstd2_ready = sem("rstd2_ready")
        wt_done = sem("wt_done")
        gw_hi, gw_ready = sem("gw_hi"), sem("gw_ready")
        w_hi, w_ready = sem("w_hi"), sem("w_ready")
        be2_hi, be2_ready = sem("be2_hi"), sem("be2_ready")
        small_ready = sem("small_ready")
        xh_ready = sem("xh_ready")
        xt_done = sem("xt_done")
        xth_ready = sem("xth_ready")
        xtl_ready = sem("xtl_ready")
        gate_done = sem("gate_done")
        r_step = sem("r_step")
        logit_ready, e_ready = sem("logit_ready"), sem("e_ready")
        cc_ready = sem("cc_ready")
        ct_done = sem("ct_done")
        ct_ready = sem("ct_ready")
        h_done = sem("h_done")
        c_done = sem("c_done")
        silu_done = sem("silu_done")
        spread_out = sem("spread_out")
        u_done = sem("u_done")
        hid_done = sem("hid_done")
        w2_done = sem("w2_done")
        y_out = sem("y_out")
        yt_done = sem("yt_done")
        out_ready = sem("out_ready")
        out_sent = sem("out_sent")

        x_v = x.rearrange("(n p) d -> p n d", p=P)
        c_v = ctx_in.rearrange("(n p) d -> p n d", p=P)
        out_v = out.rearrange("(b n p) d -> b p n d", p=P, n=TPB)

        def wait(eng, s, value):
            if not (isinstance(value, int) and value <= 0):
                eng.wait_ge(s, value)

        def back(b, j, steps, per):
            return b + (j - steps) // per, (j - steps) % per

        def exists(b):
            return not isinstance(b, int) or 0 <= b < B

        def batches(eng, body):
            body(0)
            with eng.Fori(1, B - 1) as b:
                body(b)
            body(B - 1)
            body(B)

        block = ctx.enter_context(nc.Block())

        @block.sync
        def _(sp):
            sp.dma_start(xs[:, 0:TPB, :], x_v[:, 0:TPB, :]).then_inc(x0_in, 16)
            sp.dma_start(cs[:, 0:TPB, :], c_v[:, 0:TPB, :]).then_inc(c0_in, 16)
            sp.dma_start(xs[:, TPB:TILES, :], x_v[:, TPB:TILES, :]).then_inc(xr_in, 16)
            sp.dma_start(cs[:, TPB:TILES, :], c_v[:, TPB:TILES, :]).then_inc(cr_in, 16)
            sp.dma_start(gwr[:, :], gate_w).then_inc(small_in, 16)
            sp.dma_start(brow[0:RCH, :], be1.rearrange("(c e) i -> c (e i)", e=EPC)).then_inc(small_in, 16)
            sp.dma_start(brow[RCH:CH, :], bs1.rearrange("(a n) -> a n", a=1)).then_inc(small_in, 16)
            sp.dma_start(brow[CH:CH + RCH, :], be3.rearrange("(c e) i -> c (e i)", e=EPC)).then_inc(small_in, 16)
            sp.dma_start(brow[CH + RCH:2 * CH, :], bs3.rearrange("(a n) -> a n", a=1)).then_inc(small_in, 16)
            sp.dma_start(brow[2 * CH:NB1, :], bs2.rearrange("(a n) -> a n", a=1)).then_inc(small_in, 16)
            for part in range(3):
                sp.dma_start(be2f[part * E:(part + 1) * E, :], be2).then_inc(small_in, 16)
            sp.dma_start(spreadf[:, :], spread_in).then_inc(small_in, 16)
            sp.dma_start(w13[:, 0, 0:RCH, :].rearrange("p c (e i) -> p (c e) i", e=EPC),
                         We1.rearrange("e d i -> d e i")).then_inc(w13_in, 16)
            sp.dma_start(w13[:, 1, 0:RCH, :].rearrange("p c (e i) -> p (c e) i", e=EPC),
                         We3.rearrange("e d i -> d e i")).then_inc(w13_in, 16)
            sp.dma_start(w13[:, 0, RCH, :], ws1).then_inc(w13_in, 16)
            sp.dma_start(w13[:, 1, RCH, :], ws3).then_inc(w13_in, 16)
            sp.dma_start(w2[:, 0:RCH, :], We2.rearrange("(c e) i d -> (e i) c d", e=EPC)).then_inc(w2_in, 16)
            sp.dma_start(w2[:, RCH, :], ws2).then_inc(w2_in, 16)
            with sp.Fori(0, B) as b:
                sp.wait_ge(out_ready, b + 1)
                sp.dma_start(out_v[b], outb[:, :, :]).then_inc(out_sent, 16)
            sp.wait_ge(out_sent, 16 * B)

        @block.gpsimd
        def _(pool):
            g = nc.gpsimd

            def parts(b, half, src, rest, cat, places, step, built):
                high, middle, low = places
                v = src[:, half, :, :].rearrange("p n (h d) -> p (n h) d", d=DH)
                rows = cat[:, half, :, :, :].rearrange("p n h r -> p (n h) r")[:, :, 0:QK].rearrange(
                    "p h (c d) -> p h c d", d=DH)

                def at(first, stride, copies):
                    return rows[:, :, first:first + stride * (copies - 1) + 1:stride, :]

                def copy(where, value):
                    return g.tensor_scalar(at(*where), value.unsqueeze(2).to_broadcast(
                        [P, TPB * HPH, where[2], DH]), 1.0, 1.0, ALU.mult, ALU.mult)

                n = 3 * (HALVES * b + half)
                copy(high, v).then_inc(step, 1)
                pool.wait_ge(step, n + 1)
                g.tensor_tensor(rest[:, :, :], v, rows[:, :, high[0], :], ALU.subtract).then_inc(step, 1)
                pool.wait_ge(step, n + 2).then_inc(pool_passed, 1)
                copy(middle, rest[:, :, :]).then_inc(step, 1)
                pool.wait_ge(step, n + 3)
                g.tensor_tensor(rows[:, :, low, :], rest[:, :, :], rows[:, :, middle[0], :],
                                ALU.subtract).then_inc(built, 1)

            def build_q(b, half):
                if not isinstance(b, int) or b > 0:
                    pool.wait_ge(t2_done, UPB * (b - 1) + 2 * half + 2).then_inc(pool_passed, 1)
                pool.wait_ge(qhat_ready, b + 1).then_inc(pool_passed, 1)
                parts(b, half, qhat, qrest, qcat, ((0, 1, 3), (3, 1, 2), 5), q_step, q_built)

            def build_k(b, half):
                if not isinstance(b, int) or b > 0:
                    pool.wait_ge(t_done, UPB * (b - 1) + 2 * half + 2).then_inc(pool_passed, 1)
                pool.wait_ge(kin_ready, b + 1).then_inc(pool_passed, 1)
                parts(b, half, kin, krest, kcat, ((1, 2, 3), (2, 2, 2), 0), k_step, k_built)

            def power(b):
                pool.wait_ge(var_ready, b + 1)
                wait(pool, qhat_ready, b)
                g.tensor_tensor(rstd[:, :], var8[:, :], minus_half[:, 0:TPB], ALU.pow).then_inc(rstd_ready, 1)

            pool.wait_ge(half_set, 1)
            pool.wait_ge(rows_set, 1)
            build_k(0, 0)
            power(0)
            build_q(0, 0)
            build_k(0, 1)

            def body(b):
                for j in range(UPB):
                    if j == 0 and exists(b):
                        build_q(b, 1)
                        if exists(b + 1):
                            power(b + 1)
                    if j == 1 and exists(b + 1):
                        build_k(b + 1, 0)
                    if j == 2 and exists(b + 1):
                        build_q(b + 1, 0)
                    if j == 3 and exists(b + 1):
                        build_k(b + 1, 1)

            batches(pool, body)

            for half in range(2):
                part = slice(half * TILES // 2, (half + 1) * TILES // 2)
                pool.wait_ge(var2_ready, half + 1)
                g.tensor_tensor(rstd2[:, part], var2[:, part], minus_half[:, part], ALU.pow).then_inc(rstd2_ready, 1)
            for m in range(2):
                pool.wait_ge(w_hi, m + 1)
                g.tensor_tensor(w13l[:, m, :, :], w13[:, m, :, :], w13h[:, m, :, :].bitcast(F32),
                                ALU.subtract).then_inc(w_ready, 1)
            pool.wait_ge(be2_hi, 1)
            low = slice(2 * E, 3 * E)
            pool.wait_ge(w_ready, 2)
            g.tensor_tensor(be2r[low, :], be2f[low, :], be2r[low, :].bitcast(F32), ALU.subtract).then_inc(be2_ready, 1)

            pool.wait_ge(be2_ready, 1)
            def experts(b):
                for k in range(RCH):
                    if not exists(b):
                        continue
                    slot = k % SLOTS
                    pool.wait_ge(u_done, CH * b + k + 1)
                    pool.wait_ge(spread_out, RCH * b + k + 1)
                    wait(pool, w2_done, CH * b + k - SLOTS + 1)
                    g.tensor_tensor(hid[:, slot, :], u[:, slot, :], spreadc[:, slot, :], ALU.mult).then_inc(hid_done, 1)

            batches(pool, experts)

        @block.vector
        def _(dve):
            v = nc.vector
            v.memset(minus_half[:, :], -0.5).then_inc(half_set, 1)
            v.memset(ones[:, :], 1.0).then_inc(ones_set, 1)

            def tiles(b):
                return bass.ds(TPB * b, TPB)

            def make_kin(b):
                if isinstance(b, int) and b == 0:
                    dve.wait_ge(c0_in, 16)
                if isinstance(b, int) and b == 1:
                    dve.wait_ge(cr_in, 16)
                wait(dve, k_built, HALVES * b)
                v.tensor_copy(kin[:, :, :, :], cs[:, tiles(b), :].rearrange(
                    "p n (f e) -> p f n e", f=HALVES)).then_inc(kin_ready, 1)

            def make_stats(b):
                if isinstance(b, int) and b == 0:
                    dve.wait_ge(x0_in, 16)
                if isinstance(b, int) and b == 1:
                    dve.wait_ge(xr_in, 16)
                for n in range(TPB):
                    last = v.bn_stats(stats[:, n, :], xs[:, bass.ds(TPB * b + n, 1), :])
                last.then_inc(stat_done, 1)
                dve.wait_ge(stat_done, b + 1).then_inc(dve_passed, 1)
                for n in range(TPB):
                    last = v.bn_aggr(mv[:, n, :], stats[:, n, :])
                last.then_inc(aggr_done, 1)
                dve.wait_ge(aggr_done, b + 1)
                wait(dve, rstd_ready, b)
                v.tensor_scalar(var8[:, :], mv[:, :, 1], EPS, float(DH), ALU.add, ALU.mult).then_inc(var_ready, 1)

            def make_qhat(b):
                dve.wait_ge(rstd_ready, b + 1)
                wait(dve, q_built, HALVES * b)
                for n in range(TPB):
                    last = v.tensor_scalar(qhat[:, :, n, :], xs[:, bass.ds(TPB * b + n, 1), :].rearrange(
                        "p n (f e) -> p (n f) e", f=HALVES), mv[:, n, 0:1], rstd[:, n:n + 1], ALU.subtract, ALU.mult)
                last.then_inc(qhat_ready, 1)

            def make_v(b, half):
                wait(dve, av_done, UPB * (b - 1) + 2 * half + 2)
                src = cs[:, tiles(b), :].rearrange("p n (f h d) -> p n f h d", f=HALVES, d=DH)
                v.tensor_copy(vcat[:, half, :, :, 0:DH], src[:, :, half, :, :]).then_inc(v_ready, 1)

            def second_q(b, j):
                n = UPB * b + j
                dve.wait_ge(t2_done, n + 1)
                wait(dve, st_done, 2 * n)
                v.tensor_copy(q2T[:, :, :], ps_t2).then_inc(q2_ready, 1)

            def maximum(b, j, a):
                dve.wait_ge(s_done, 2 * (UPB * b + j) + a + 1)
                v.tensor_reduce(negmax[:, j % 2, 0, 2 * a:2 * a + 2], bank_s[:, :, 0:P], AX_X, ALU.max, negate=True)
                v.tensor_reduce(negmax[:, j % 2, 1, 2 * a:2 * a + 2], bank_s[:, :, P:3 * P], AX_X, ALU.max,
                                negate=True).then_inc(max_done, 1)

            def shift_rows(j):
                half, first = j // 2, (j % 2) * HPU
                return [qcat[:, half, :, first:first + HPU, R_MAX + part] for part in range(2)]

            def body(b):
                for j in range(UPB):
                    pb, pj = back(b, j, 1, UPB)
                    ob, oj = back(b, j, 4, UPB)
                    on = UPB * ob + oj
                    o = bank_ot[:, 0, 0:SEQ].rearrange("p (n h w) -> p n h w", n=TPB, w=QUAD)
                    if exists(b):
                        maximum(b, j, 0)
                    if exists(pb):
                        second_q(pb, pj)
                    if exists(b):
                        maximum(b, j, 1)
                        row_hi, row_lo = shift_rows(j)
                        dve.wait_ge(max_done, 2 * (UPB * b + j) + 2)
                        v.tensor_copy(row_hi, negmax[:, j % 2, :, :]).then_inc(chi_done, 1)
                    if exists(ob):
                        dve.wait_ge(ot_done, on + 1)
                        v.reciprocal(rsum[:, :, :], o[:, :, :, DH]).then_inc(recip_done, 1)
                    if exists(b):
                        dve.wait_ge(chi_done, UPB * b + j + 1)
                        v.tensor_tensor(row_lo, negmax[:, j % 2, :, :], row_hi, ALU.subtract).then_inc(c_ready, 1)
                    if exists(ob):
                        dve.wait_ge(recip_done, on + 1)
                        v.tensor_tensor(onorm[:, :, :].rearrange("p n (h d) -> p n h d", d=DH), o[:, :, :, 0:DH],
                                        rsum[:, :, :].unsqueeze(3).to_broadcast([P, TPB, HPU, DH]),
                                        ALU.mult).then_inc(o_read, 1)
                        dve.wait_ge(o_read, on + 1)
                        columns = slice(oj * HPU * DH, (oj + 1) * HPU * DH)
                        v.scalar_tensor_tensor(xs[:, tiles(ob), columns], onorm[:, :, :], tg[:, 0:1],
                                               xs[:, tiles(ob), columns], ALU.mult, ALU.add).then_inc(x1_ready, 1)
                    if j == 0 and exists(b + 1):
                        make_stats(b + 1)
                        make_kin(b + 1)
                    if j == 1 and exists(b + 1):
                        make_qhat(b + 1)
                    if j in (0, 2) and exists(b):
                        make_v(b, j // 2)

            make_kin(0)
            qrows = qcat[:, :, :, :, :].rearrange("p f n h r -> p (f n h) r")
            krows = kcat[:, :, :, :, :].rearrange("p f n h r -> p (f n h) r")
            v.memset(qrows[:, :, R_MAX:ROWS], 0.0)
            v.memset(krows[:, :, R_MAX:K_ST], 1.0)
            v.memset(krows[:, :, K_ST:ROWS], 0.0)
            make_stats(0)
            dve.wait_ge(cst_in, 16)
            for half in range(HALVES):
                slopes = cst[:, C_SLOPE + half * 3 * HPH:C_SLOPE + (half + 1) * 3 * HPH].rearrange(
                    "p (h c) -> p h c", c=3)
                for n in range(TPB):
                    v.tensor_copy(qcat[:, half, n, :, R_SLOPE:R_MAX], slopes)
            for n in range(TPB):
                last = v.tensor_copy(kcat[:, :, n, :, R_SLOPE:R_MAX],
                                     cst[:, C_POS + n:C_POS + n + 1].unsqueeze(2).unsqueeze(3).to_broadcast(
                                         [P, HALVES, HPH, 3]))
            last.then_inc(rows_set, 1)
            v.tensor_copy(identb[:, :], ident)
            v.tensor_copy(maskb[:, :], cst[:, C_MASK:C_MASK + P]).then_inc(consts_set, 1)
            make_qhat(0)
            v.memset(vcat[:, :, :, :, :], 0.0).then_inc(rows_set, 1)
            dve.wait_ge(rows_set, 2)
            v.memset(vcat[:, :, :, :, DH].rearrange("p f n h -> p (f n) h"), 1.0)
            dve.wait_ge(tg_ready, 1)
            batches(dve, body)

            dve.wait_ge(x1_ready, UNITS)
            for half in range(2):
                part = range(half * TILES // 2, (half + 1) * TILES // 2)
                for n in part:
                    last = v.bn_stats(stats2[:, n, :], xs[:, n, :])
                last.then_inc(stat2_done, 1)
                dve.wait_ge(stat2_done, half + 1)
                for n in part:
                    last = v.bn_aggr(mv2[:, n, :], stats2[:, n, :])
                last.then_inc(aggr2_done, 1)
                dve.wait_ge(aggr2_done, half + 1)
                v.tensor_scalar(var2[:, part.start:part.stop], mv2[:, part.start:part.stop, 1], EPS, None,
                                ALU.add).then_inc(var2_ready, 1)
            dve.wait_ge(gw_hi, 1)
            v.tensor_tensor(gwT[:, 1, :], ps_w[:, 0:E], gwT[:, 0, :].bitcast(F32), ALU.subtract).then_inc(gw_ready, 1)

            def low(gr):
                dve.wait_ge(xth_ready, gr + 1)
                at = slice(gr * GT * P, (gr + 1) * GT * P)
                v.tensor_tensor(xTl[:, at], ps_xt[gr % 2], xTh[:, at].bitcast(F32), ALU.subtract).then_inc(xtl_ready, 1)

            for gr in range(NG):
                dve.wait_ge(rstd2_ready, gr * GT // (TILES // 2) + 1)
                wait(dve, xt_done, gr - 1)
                for n in range(GT):
                    t = gr * GT + n
                    last = v.tensor_scalar(xh[:, gr % 2, n, :], xs[:, t, :], mv2[:, t, 0:1], rstd2[:, t:t + 1],
                                           ALU.subtract, ALU.mult)
                last.then_inc(xh_ready, 1)
                if gr > 0:
                    low(gr - 1)
            low(NG - 1)

            shift, shifted, e_val, p_val, biased, limited, work, hot1, hot2 = (
                [one[:, 0, :]] + [wide[:, n, :, :] for n in range(8)])
            total, inv, best, first = (one[:, n, :] for n in range(1, 5))
            per_e = [P, TILES, E]

            def over_e(value):
                return value.unsqueeze(2).to_broadcast(per_e)

            step = count(1)
            dve.wait_ge(gate_done, 1)
            v.tensor_reduce(shift, ps_logit, AX_X, ALU.max, negate=True).then_inc(r_step, 1)
            dve.wait_ge(r_step, next(step))
            v.tensor_tensor(shifted, ps_logit, over_e(shift), ALU.add).then_inc(logit_ready, 1)
            dve.wait_ge(e_ready, 1)
            v.tensor_reduce(total, e_val, AX_X, ALU.add).then_inc(r_step, 1)
            dve.wait_ge(r_step, next(step))
            v.reciprocal(inv, total).then_inc(r_step, 1)
            dve.wait_ge(r_step, next(step))
            v.tensor_tensor(p_val, e_val, over_e(inv), ALU.mult).then_inc(r_step, 1)
            dve.wait_ge(r_step, next(step))
            v.tensor_tensor(biased, p_val, gateb[:, :].unsqueeze(1).to_broadcast(per_e), ALU.add).then_inc(r_step, 1)
            dve.wait_ge(r_step, next(step))
            quads = biased.rearrange("p n (g c) -> p (n g) c", c=E // GROUPS)
            hi2, lo2 = minmax[:, 0, :, :], minmax[:, 1, :, :]
            top1, mid1, mid2, top2, score, lack = (
                narrow[:, n, :, :].rearrange("p n g -> p (n g)") for n in range(6))
            v.tensor_tensor(hi2, quads[:, :, 0:2], quads[:, :, 2:4], ALU.max)
            v.tensor_tensor(lo2, quads[:, :, 0:2], quads[:, :, 2:4], ALU.min).then_inc(r_step, 1)
            dve.wait_ge(r_step, next(step))
            v.tensor_tensor(top1, hi2[:, :, 0], hi2[:, :, 1], ALU.max)
            v.tensor_tensor(mid1, hi2[:, :, 0], hi2[:, :, 1], ALU.min)
            v.tensor_tensor(mid2, lo2[:, :, 0], lo2[:, :, 1], ALU.max).then_inc(r_step, 1)
            dve.wait_ge(r_step, next(step))
            v.tensor_tensor(top2, mid1, mid2, ALU.max).then_inc(r_step, 1)
            dve.wait_ge(r_step, next(step))
            v.tensor_tensor(score, top1, top2, ALU.add).then_inc(r_step, 1)
            dve.wait_ge(r_step, next(step))
            per_g = [P, TILES, GROUPS, GROUPS]
            gs = narrow[:, 4, :, :]
            other, own = gs.unsqueeze(2).to_broadcast(per_g), gs.unsqueeze(3).to_broadcast(per_g)
            larger, equal, ahead = (rank[:, n, :, :, :] for n in range(3))
            lower = cst[:, C_LOWER:C_LOWER + GROUPS * GROUPS].rearrange("p (g o) -> p g o", o=GROUPS)
            v.tensor_tensor(larger, other, own, ALU.is_gt)
            v.tensor_tensor(equal, other, own, ALU.is_equal).then_inc(r_step, 1)
            dve.wait_ge(r_step, next(step))
            v.tensor_tensor(ahead, equal, lower.unsqueeze(1).to_broadcast(per_g), ALU.mult).then_inc(r_step, 1)
            dve.wait_ge(r_step, next(step))
            v.tensor_tensor(equal, larger, ahead, ALU.add).then_inc(r_step, 1)
            dve.wait_ge(r_step, next(step))
            v.tensor_reduce(narrow[:, 5, :, :], equal, AX_X, ALU.add).then_inc(r_step, 1)
            dve.wait_ge(r_step, next(step))
            v.tensor_scalar(narrow[:, 6, :, :], narrow[:, 5, :, :], KEEP_GROUPS - 0.5, MASKED, ALU.is_gt,
                            ALU.mult).then_inc(r_step, 1)
            dve.wait_ge(r_step, next(step))
            v.tensor_tensor(limited.rearrange("p n (g c) -> p (n g) c", g=GROUPS), quads,
                            narrow[:, 6, :, :].rearrange("p n g -> p (n g)").unsqueeze(2).to_broadcast(
                                [P, TILES * GROUPS, E // GROUPS]), ALU.add).then_inc(r_step, 1)
            dve.wait_ge(r_step, next(step))
            descending = cst[:, C_E:C_E + E].unsqueeze(1).to_broadcast(per_e)
            for hot in (hot1, hot2):
                v.tensor_reduce(best, limited, AX_X, ALU.max).then_inc(r_step, 1)
                dve.wait_ge(r_step, next(step))
                v.tensor_tensor(work, limited, over_e(best), ALU.is_equal).then_inc(r_step, 1)
                dve.wait_ge(r_step, next(step))
                v.tensor_tensor(shifted, work, descending, ALU.mult).then_inc(r_step, 1)
                dve.wait_ge(r_step, next(step))
                v.tensor_reduce(first, shifted, AX_X, ALU.max).then_inc(r_step, 1)
                dve.wait_ge(r_step, next(step))
                v.tensor_tensor(hot, over_e(first), descending, ALU.is_equal).then_inc(r_step, 1)
                dve.wait_ge(r_step, next(step))
                if hot is hot1:
                    v.scalar_tensor_tensor(limited, hot1, MASKED, limited, ALU.mult, ALU.add).then_inc(r_step, 1)
                    dve.wait_ge(r_step, next(step))
            v.tensor_tensor(work, hot1, hot2, ALU.add).then_inc(r_step, 1)
            dve.wait_ge(r_step, next(step))
            v.tensor_tensor(shifted, work, p_val, ALU.mult).then_inc(r_step, 1)
            dve.wait_ge(r_step, next(step))
            v.tensor_copy(c_hi[:, :, :], shifted).then_inc(r_step, 1)
            dve.wait_ge(r_step, next(step))
            v.tensor_copy(ccat[:, :, 0:3:2, :], c_hi[:, :, :].bitcast(F32).unsqueeze(2).to_broadcast([P, TILES, 2, E]))
            v.tensor_tensor(ccat[:, :, 1, :], shifted, c_hi[:, :, :].bitcast(F32), ALU.subtract).then_inc(cc_ready, 1)

            dve.wait_ge(small_ready, 1)
            def experts(b):
                for k in range(CH):
                    pb = b - 1
                    if k == 4 and exists(pb):
                        dve.wait_ge(yt_done, pb + 1)
                        v.scalar_tensor_tensor(outb[:, :, :], ps_yt.rearrange("p (n d) -> p n d", n=TPB), tg[:, 1:2],
                                               xs[:, tiles(pb), :], ALU.mult, ALU.add).then_inc(out_ready, 1)
                    if not exists(b):
                        continue
                    if k == RCH and exists(pb):
                        dve.wait_ge(out_sent, 16 * (pb + 1))
                    c = CH * b + k
                    dve.wait_ge(silu_done, c + 1)
                    ub, uk = back(b, k, SLOTS, CH)
                    wait(dve, hid_done, RCH * ub + min(uk + 1, RCH))
                    target = u
                    if k == RCH:
                        target = hid
                        wait(dve, w2_done, c - SLOTS + 1)
                    v.scalar_tensor_tensor(target[:, k % SLOTS, :], ps_h[k % SLOTS][:, SEQ:2 * SEQ],
                                           bcol[:, CH + k:CH + k + 1], s1[:, k % SLOTS, :],
                                           ALU.add, ALU.mult).then_inc(u_done, 1)

            batches(dve, experts)

        @block.scalar
        def _(act):
            s = nc.scalar
            act.dma_start(cst[:, :], const_in).then_inc(cst_in, 16)
            act.dma_start(gl[:, 0:1], g_xattn.rearrange("(a n) -> a n", a=1)).then_inc(gl_in, 16)
            act.dma_start(gl[:, 1:2], g_ffn.rearrange("(a n) -> a n", a=1)).then_inc(gl_in, 16)
            act.dma_start(gl[:, 2:2 + E], gate_b.rearrange("(a n) -> a n", a=1)).then_inc(gl_in, 16)
            act.wait_ge(gl_done, 1)
            s.activation(tg[:, :], bank_ot[:, 0, 0:2], ACT.Tanh)
            s.copy(gateb[:, :], bank_ot[:, 0, 2:2 + E]).then_inc(tg_ready, 1)

            def operands(b, j):
                n = UPB * b + j
                act.wait_ge(t_done, n + 1)
                wait(act, st_done, 2 * (n - UPB) + 2)
                s.copy(qkT[:, j, :, :], ps_t).then_inc(qk_ready, 1)

            def exponent(b, j, a):
                n = UPB * b + j
                act.wait_ge(st_done, 2 * n + a + 1)
                wait(act, av_done, n - 1)
                s.activation(prob[:, j % 2, 2 * a:2 * a + 2, :], bank_st[:, :, 0:3 * P], ACT.Exp).then_inc(exp_done, 1)

            def outputs(b, j):
                n = UPB * b + j
                act.wait_ge(av_done, n + 1)
                wait(act, ot_done, n - 1)
                s.copy(avT[:, j % 2, :], bank_av[:, 0, 0:SEQ]).then_inc(av_out, 1)

            operands(0, 0)

            def body(b):
                for j in range(UPB):
                    nb, nj = back(b, j, -1, UPB)
                    pb, pj = back(b, j, 1, UPB)
                    ab, aj = back(b, j, 2, UPB)
                    if exists(b) and exists(nb):
                        operands(nb, nj)
                    if exists(pb):
                        exponent(pb, pj, 0)
                    if exists(ab):
                        outputs(ab, aj)
                    if exists(pb):
                        exponent(pb, pj, 1)

            batches(act, body)

            act.wait_ge(wt_done, 1)
            s.copy(bcol[:, :], ps_w[:, E:E + NB1])
            s.copy(gwT[:, 0, :], ps_w[:, 0:E]).then_inc(gw_hi, 1)
            act.wait_ge(w13_in, 16 * 4)
            for m in range(2):
                s.copy(w13h[:, m, :, :], w13[:, m, :, :]).then_inc(w_hi, 1)
            act.wait_ge(small_in, 16 * 10)
            s.copy(be2r[:, :], be2f[:, :]).then_inc(be2_hi, 1)
            s.copy(spreadr[:, :], spreadf[:, :]).then_inc(small_ready, 1)
            for gr in range(NG):
                act.wait_ge(xt_done, gr + 1)
                s.copy(xTh[:, gr * GT * P:(gr + 1) * GT * P], ps_xt[gr % 2]).then_inc(xth_ready, 1)
            act.wait_ge(logit_ready, 1)
            s.activation(wide[:, 1, :, :], wide[:, 0, :, :], ACT.Exp).then_inc(e_ready, 1)
            for gr in range(NG):
                act.wait_ge(ct_done, gr + 1)
                s.copy(cT[:, gr * GT * P:(gr + 1) * GT * P], ps_ct[gr % 2]).then_inc(ct_ready, 1)

            def experts(b):
                for k in range(CH):
                    if k == 2 and exists(b - 1):
                        act.wait_ge(w2_done, CH * b)
                        s.activation(yT[:, :], ps_y, ACT.Identity, bias=bcol[:, 2 * CH:NB1]).then_inc(y_out, 1)
                    if not exists(b):
                        continue
                    c, slot = CH * b + k, k % SLOTS
                    act.wait_ge(h_done, c + 1)
                    wait(act, u_done, c - SLOTS + 1)
                    s.activation(s1[:, slot, :], ps_h[slot][:, 0:SEQ], ACT.Silu,
                                 bias=bcol[:, k:k + 1]).then_inc(silu_done, 1)
                    if k < RCH:
                        cb, ck = back(b, k, SLOTS, CH)
                        act.wait_ge(c_done, RCH * b + k + 1)
                        wait(act, hid_done, RCH * cb + min(ck + 1, RCH))
                        s.copy(spreadc[:, slot, :], ps_c[slot][:, 0:SEQ]).then_inc(spread_out, 1)

            batches(act, experts)

        @block.tensor
        def _(pe):
            mm, transpose = nc.tensor.matmul, nc.tensor.transpose
            mask = maskb[:, :].unsqueeze(1).to_broadcast([P, 2, P])
            eye = identb[:, :].unsqueeze(1).to_broadcast([P, 2, P])

            def transposed(b, j):
                n, half, first = UPB * b + j, j // 2, (j % 2) * HPU
                pe.wait_ge(q_built, HALVES * b + half + 1)
                pe.wait_ge(k_built, HALVES * b + half + 1)
                wait(pe, qk_ready, n)
                for a in range(2):
                    for which, cat in enumerate((qcat, kcat)):
                        for t in range(TPB):
                            at = (which * TPB + t) * P
                            last = transpose(ps_t[:, a, at:at + P], cat[:, half, t, first + 2 * a:first + 2 * a + 2, :]
                                             .rearrange("p h r -> p (h r)"), identb[:, :])
                last.then_inc(t_done, 1)

            def scores(b, j, a):
                n = UPB * b + j
                pe.wait_ge(qk_ready, n + 1)
                wait(pe, max_done, 2 * n + a)
                for p in range(2):
                    rows = slice(p * ROWS, p * ROWS + K_S)
                    q, k = qkT[rows, j, a, 0:SEQ], qkT[rows, j, a, SEQ:2 * SEQ]
                    diagonal = bank_s[:, p, 0:3 * P].rearrange("p (x n) -> p x n", n=P)[:, 0:3:2, :]
                    mm(diagonal, identb[:, :], mask, start=True, stop=False, skip_group_check=True)
                    mm(bank_s[:, p, 0:P], q[:, 0:P], k[:, 0:P], start=False, stop=True, skip_group_check=True)
                    last = mm(bank_s[:, p, P:3 * P], q[:, P:SEQ], k, start=False, stop=True, skip_group_check=True)
                last.then_inc(s_done, 1)

            def second(b, j):
                n, half, first = UPB * b + j, j // 2, (j % 2) * HPU
                pe.wait_ge(c_ready, n + 1)
                wait(pe, q2_ready, n)
                for a in range(2):
                    for t in range(TPB):
                        last = transpose(ps_t2[:, a, t * P:(t + 1) * P], qcat[:, half, t, first + 2 * a:first + 2 * a + 2, :]
                                         .rearrange("p h r -> p (h r)"), identb[:, :])
                last.then_inc(t2_done, 1)

            def scores_t(b, j, a):
                n = UPB * b + j
                pe.wait_ge(q2_ready, n + 1)
                wait(pe, exp_done, 2 * n + a)
                for p in range(2):
                    rows = slice(p * ROWS, p * ROWS + K_ST)
                    k = qkT[rows, j, a, SEQ:2 * SEQ]
                    diagonal = bank_st[:, p, 0:3 * P].rearrange("p (x n) -> p x n", n=P)[:, 0:3:2, :]
                    mm(diagonal, maskb[:, :], eye, start=True, stop=False, skip_group_check=True)
                    mm(bank_st[:, p, 0:SEQ], k[:, 0:P], q2T[rows, a, :], start=False, stop=True, skip_group_check=True)
                    last = mm(bank_st[:, p, SEQ:3 * P], k[:, P:SEQ], q2T[rows, a, P:SEQ], start=False, stop=True,
                              skip_group_check=True)
                last.then_inc(st_done, 1)

            def values(b, j):
                n, half, first = UPB * b + j, j // 2, (j % 2) * HPU
                pe.wait_ge(exp_done, 2 * n + 2)
                pe.wait_ge(v_ready, HALVES * b + half + 1)
                wait(pe, av_out, n)
                for h in range(HPU):
                    mm(bank_av[h * QUAD:(h + 1) * QUAD, 0, 0:SEQ], vcat[:, half, 0, first + h, :],
                       prob[:, j % 2, h, 0:SEQ], start=True, stop=False, skip_group_check=True,
                       tile_position=(0, h * QUAD))
                for h in range(HPU):
                    last = mm(bank_av[h * QUAD:(h + 1) * QUAD, 0, P:SEQ], vcat[:, half, 1, first + h, :],
                              prob[:, j % 2, h, SEQ:3 * P], start=False, stop=True, skip_group_check=True,
                              tile_position=(0, h * QUAD))
                last.then_inc(av_done, 1)

            def outputs(b, j):
                n = UPB * b + j
                pe.wait_ge(av_out, n + 1)
                wait(pe, o_read, n)
                for t in range(TPB):
                    last = transpose(bank_ot[:, 0, t * P:(t + 1) * P], avT[:, j % 2, t * P:(t + 1) * P], ident)
                last.then_inc(ot_done, 1)

            pe.wait_ge(ones_set, 1)
            pe.wait_ge(gl_in, 16 * 3)
            mm(bank_ot[:, 0, 0:2 + E], ones[:, :], gl[:, :], start=True, stop=True).then_inc(gl_done, 1)
            pe.wait_ge(consts_set, 1)
            transposed(0, 0)

            def body(b):
                for j in range(UPB):
                    nb, nj = back(b, j, -1, UPB)
                    pb, pj = back(b, j, 1, UPB)
                    ab, aj = back(b, j, 2, UPB)
                    ob, oj = back(b, j, 3, UPB)
                    if exists(b):
                        scores(b, j, 0)
                    if exists(pb):
                        second(pb, pj)
                    if exists(b) and exists(nb):
                        transposed(nb, nj)
                    if exists(b):
                        scores(b, j, 1)
                    if exists(pb):
                        scores_t(pb, pj, 0)
                    if exists(ab):
                        values(ab, aj)
                    if exists(pb):
                        scores_t(pb, pj, 1)
                    if exists(ob):
                        if isinstance(b, int) and b == 0:
                            pe.wait_ge(tg_ready, 1)
                        outputs(ob, oj)

            batches(pe, body)

            pe.wait_ge(small_in, 16 * 10)
            transpose(ps_w[:, 0:E], gwr[:, :], ident[0:E, 0:E])
            transpose(ps_w[:, E:E + NB1], brow[:, :], ident[0:NB1, 0:NB1]).then_inc(wt_done, 1)

            def logits(gr):
                pe.wait_ge(xtl_ready, gr + 1)
                for t in range(gr * GT, (gr + 1) * GT):
                    at = slice(t * P, (t + 1) * P)
                    mm(ps_logit[:, t, :], xTh[:, at], gwT[:, 0, :], start=True, stop=False, skip_group_check=True)
                    mm(ps_logit[:, t, :], xTh[:, at], gwT[:, 1, :], start=False, stop=False, skip_group_check=True)
                    last = mm(ps_logit[:, t, :], xTl[:, at], gwT[:, 0, :], start=False, stop=True,
                              skip_group_check=True)
                return last

            pe.wait_ge(gw_ready, 1)
            for gr in range(NG):
                pe.wait_ge(xh_ready, gr + 1)
                wait(pe, xtl_ready, gr - 1)
                for n in range(GT):
                    last = transpose(ps_xt[gr % 2][:, n * P:(n + 1) * P], xh[:, gr % 2, n, :], ident)
                last.then_inc(xt_done, 1)
                if gr > 0:
                    logits(gr - 1)
            logits(NG - 1).then_inc(gate_done, 1)
            pe.wait_ge(cc_ready, 1)
            for gr in range(NG):
                wait(pe, ct_ready, gr - 1)
                for n in range(GT):
                    last = transpose(ps_ct[gr % 2][:, n * P:(n + 1) * P],
                                     ccat[:, gr * GT + n, :, :].rearrange("p c e -> p (c e)"), ident)
                last.then_inc(ct_done, 1)

            pe.wait_ge(w_ready, 2)
            pe.wait_ge(be2_ready, 1)
            pe.wait_ge(small_ready, 1)
            pe.wait_ge(ct_ready, NG)
            pe.wait_ge(w2_in, 16 * 2)

            def hidden(b, k):
                slot, tokens = k % SLOTS, bass.ds(SEQ * b, SEQ)
                cb, ck = back(b, k, SLOTS, CH)
                wait(pe, spread_out, RCH * cb + min(ck + 1, RCH))
                wait(pe, u_done, CH * b + k - SLOTS + 1)
                for m in range(2):
                    target = ps_h[slot][:, m * SEQ:(m + 1) * SEQ]
                    mm(target, w13h[:, m, k, :], xTh[:, tokens], start=True, stop=False, skip_group_check=True)
                    mm(target, w13h[:, m, k, :], xTl[:, tokens], start=False, stop=False, skip_group_check=True)
                    last = mm(target, w13l[:, m, k, :], xTh[:, tokens], start=False, stop=True, skip_group_check=True)
                last.then_inc(h_done, 1)
                if k < RCH:
                    mm(ps_c[slot][:, 0:SEQ], spreadr[:, k * P:(k + 1) * P], cT[0:2 * E, tokens],
                       start=True, stop=True).then_inc(c_done, 1)

            def down(b, k):
                if k == 0:
                    wait(pe, y_out, b)
                if k < RCH:
                    pe.wait_ge(hid_done, RCH * b + k + 1)
                else:
                    pe.wait_ge(u_done, CH * b + k + 1)
                last = mm(ps_y, w2[:, k, :], hid[:, k % SLOTS, :], start=k == 0, stop=k == RCH, skip_group_check=True)
                if k == 0:
                    last = mm(ps_y, be2r[:, :], cT[:, bass.ds(SEQ * b, SEQ)], start=False, stop=False,
                              skip_group_check=True)
                last.then_inc(w2_done, 1)

            def experts(b):
                for k in range(CH):
                    if exists(b):
                        hidden(b, k)
                    db, dk = back(b, k, 2, CH)
                    if k == 3 and exists(b - 1):
                        pe.wait_ge(y_out, b)
                        for n in range(TPB):
                            last = transpose(ps_yt[:, n * P:(n + 1) * P], yT[:, n * P:(n + 1) * P], ident)
                        last.then_inc(yt_done, 1)
                    if exists(db):
                        down(db, dk)

            batches(pe, experts)


def kernel(**inputs):
    import numpy as np
    import concourse.bacc as bacc
    from concourse import mybir
    from concourse.bass_utils import run_bass_kernel_spmd
    nc = bacc.Bacc("TRN2", target_bir_lowering=False, num_devices=1)
    table, spread = constants()
    arrays = {"x": np.ascontiguousarray(inputs["x"]).reshape(B * SEQ, D),
              "ctx": np.ascontiguousarray(inputs["ctx_1024"]).reshape(B * SEQ, D),
              "g_xattn": np.ascontiguousarray(inputs["g_xattn"]),
              "g_ffn": np.ascontiguousarray(inputs["g_ffn"])}
    for name in ("gate_w", "gate_b", "We1", "be1", "We2", "be2", "We3", "be3", "ws1", "bs1", "ws2", "bs2", "ws3", "bs3"):
        arrays[name] = np.ascontiguousarray(inputs["L0_ffn_" + name])
    arrays["table"], arrays["spread"] = table, spread
    ins = [nc.dram_tensor(name + "_in", a.shape, mybir.dt.float32, kind="ExternalInput").ap()
           for name, a in arrays.items()]
    out = nc.dram_tensor("y_out", (B * SEQ, D), mybir.dt.float32, kind="ExternalOutput").ap()
    program(nc, *ins, out)
    res = run_bass_kernel_spmd(nc, [{name + "_in": a for name, a in arrays.items()}], core_ids=[0])
    return res.results[0]["y_out"].reshape(B, SEQ, D)
```

```python
from contextlib import ExitStack

import numpy as np

import concourse.bass as bass
from concourse import mybir

F32 = mybir.dt.float32
F32R = mybir.dt.float32r
BF16 = mybir.dt.bfloat16
ALU = mybir.AluOpType
ACT = mybir.ActivationFunctionType
AX_X = mybir.AxisListType.X

P = 128
B, SEQ, D = 8, 256, 128
TPB = SEQ // P
TILES = B * TPB
H = 16
DH = D // H
UPB = 4
HPU = H // UPB
HALVES = 2
HPH = H // HALVES
QUAD = 32
BANK = 512
UNITS = B * UPB
EPS = 1e-5
MASKED = -1e30

ROWS = 64
QK = 6 * DH
R_SLOPE = QK
R_MAX = QK + 3
K_S = QK + 3
K_ST = QK + 5

E, GROUPS, TOPK = 16, 4, 2
INTER = 64
EPC = P // INTER
RCH = E // EPC
CH = RCH + 1
KEEP_GROUPS = 2
CHOOSE_STEPS = 24
WARM_UP = 20
SLOTS = 3
NB1 = 2 * CH + 1

C_ID, C_MASK, C_SLOPE, C_POS, C_E, C_LOWER = 0, P, 2 * P, 2 * P + 3 * H, 2 * P + 3 * H + TPB, 2 * P + 3 * H + TPB + E
C_END = C_LOWER + GROUPS * GROUPS


def to_bfloat16(v):
    bits = v.view(np.uint32)
    return ((bits + 0x7FFF + ((bits >> 16) & 1)) & np.uint32(0xFFFF0000)).view(np.float32)


def constants():
    c = np.zeros((P, C_END), np.float32)
    c[:, C_ID:C_ID + P] = np.eye(P)
    t, s = np.arange(P)[:, None], np.arange(P)[None, :]
    c[:, C_MASK:C_MASK + P] = np.where(s > t, MASKED, 0.0)
    rest = np.cumprod(np.full((H,), 2.0 ** (-8.0 / H), np.float32), dtype=np.float32)
    for part in range(3):
        piece = to_bfloat16(rest)
        c[:, C_SLOPE + part:C_SLOPE + 3 * H:3] = piece
        rest = rest - piece
    for n in range(TPB):
        c[:, C_POS + n] = np.arange(P) + n * P
    c[:, C_E:C_E + E] = E - np.arange(E)
    c[:, C_LOWER:C_END] = np.tril(np.ones((GROUPS, GROUPS)), -1).reshape(-1)
    spread = np.zeros((2 * E, RCH, P), np.float32)
    for e in range(E):
        spread[e, e // EPC, (e % EPC) * INTER:(e % EPC + 1) * INTER] = 1.0
        spread[E + e] = spread[e]
    return c, spread.reshape(2 * E, RCH * P)


def program(nc, x, ctx_in, g_xattn, g_ffn, gate_w, gate_b, We1, be1, We2, be2, We3, be3,
            ws1, bs1, ws2, bs2, ws3, bs3, const_in, spread_in, out):
    ctx = ExitStack()
    with ctx:
        def sb(name, shape, dt=F32):
            return ctx.enter_context(nc.sbuf_tensor(name, shape, dt))

        def sem(name):
            return ctx.enter_context(nc.semaphore(name))

        cst = sb("cst", [P, C_END])
        ident = cst[:, C_ID:C_ID + P]
        identb = sb("identb", [P, P], BF16)
        warm = sb("warm", [P, BANK], BF16)
        maskb = sb("maskb", [P, P], BF16)
        xs = sb("xs", [P, TILES, D])
        cs = sb("cs", [P, TILES, D])
        stats = sb("stats", [P, TPB, 6])
        mv = sb("mv", [P, TPB, 2])
        var8 = sb("var8", [P, TPB])
        minus_half = sb("minus_half", [P, TILES])
        rstd = sb("rstd", [P, TPB])
        qhat = sb("qhat", [P, HALVES, TPB, D // HALVES])
        kin = sb("kin", [P, HALVES, TPB, D // HALVES])
        qrest = sb("qrest", [P, TPB * HPH, DH])
        krest = sb("krest", [P, TPB * HPH, DH])
        qcat = sb("qcat", [P, HALVES, TPB, HPH, ROWS], BF16)
        kcat = sb("kcat", [P, HALVES, TPB, HPH, ROWS], BF16)
        vcat = sb("vcat", [P, HALVES, TPB, HPH, QUAD])
        qkT = sb("qkT", [P, UPB, 2, 2 * SEQ], BF16)
        q2T = sb("q2T", [P, 2, 2, SEQ], BF16)
        negmax = sb("negmax", [P, 2, TPB, HPU])
        prob = sb("prob", [P, 2, HPU, 3 * P])
        avT = sb("avT", [P, 2, SEQ])
        rsum = sb("rsum", [P, TPB, HPU])
        onorm = sb("onorm", [P, TPB, HPU * DH])
        gl = sb("gl", [1, 2 + E])
        ones = sb("ones", [1, P])
        tg = sb("tg", [P, 2])
        gateb = sb("gateb", [P, E])
        gwr = sb("gwr", [E, D])
        gwT = sb("gwT", [P, 2, E], F32R)
        brow = sb("brow", [NB1, P])
        bcol = sb("bcol", [P, NB1])
        w13 = sb("w13", [P, 2, CH, P])
        w13h = sb("w13h", [P, 2, CH, P], F32R)
        w13l = sb("w13l", [P, 2, CH, P], F32R)
        w2 = sb("w2", [P, CH, D])
        be2f = sb("be2f", [3 * E, D])
        be2r = sb("be2r", [3 * E, D], F32R)
        spreadf = sb("spreadf", [2 * E, RCH * P])
        spreadr = sb("spreadr", [2 * E, RCH * P], F32R)
        stats2 = sb("stats2", [P, TILES, 6])
        mv2 = sb("mv2", [P, TILES, 2])
        var2 = sb("var2", [P, TILES])
        rstd2 = sb("rstd2", [P, TILES])
        xh = sb("xh", [P, 2, TPB, D])
        xTh = sb("xTh", [P, B * SEQ], F32R)
        xTl = sb("xTl", [P, B * SEQ], F32R)
        logT = sb("logT", [E, 2, SEQ])
        wide = sb("wide", [P, 4, TILES, E])
        one = sb("one", [P, 3, TILES])
        choice = sb("choice", [P, 6, TPB, E])
        narrow = sb("narrow", [P, 7, TPB * GROUPS])
        minmax = sb("minmax", [P, 2, TPB * GROUPS, 2])
        rank = sb("rank", [P, 3, TPB, GROUPS, GROUPS])
        best = sb("best", [P, TPB])
        first_of = sb("first_of", [P, TPB])
        c_hi = sb("c_hi", [P, TPB, E], F32R)
        ccat = sb("ccat", [P, TPB, 3, E])
        cT = sb("cT", [3 * E, B * SEQ], F32R)
        s1 = sb("s1", [P, SLOTS, SEQ])
        spreadc = sb("spreadc", [P, SLOTS, SEQ])
        u = sb("u", [P, SLOTS, SEQ])
        hid = sb("hid", [P, SLOTS, SEQ])
        yT = sb("yT", [P, SEQ])
        outb = sb("outb", [P, TPB, D])

        def psum(name, banks=1):
            return ctx.enter_context(nc.psum_tensor(name, [P, banks, BANK], F32))

        bank_t, bank_t2, bank_s, bank_st, bank_av, bank_ot = (
            psum("bank_t"), psum("bank_t2"), psum("bank_s", 2), psum("bank_st", 2), psum("bank_av"), psum("bank_ot"))
        ps_t = bank_t[:, 0, :].bitcast(BF16).rearrange("p (a n) -> p a n", a=2)
        ps_t2 = bank_t2[:, 0, 0:SEQ].bitcast(BF16).rearrange("p (a n) -> p a n", a=2)
        ps_xt = [bank_t[:, 0, 0:SEQ], bank_t2[:, 0, 0:SEQ]]
        ps_logT = bank_s[0:E, 0, 0:SEQ]
        ps_logit = bank_s[:, 1, 0:TILES * E].rearrange("p (n e) -> p n e", e=E)
        ps_w = bank_s[:, 1, TILES * E:]
        ps_h = [bank_t[:, 0, :], bank_t2[:, 0, :], bank_s[:, 0, :]]
        ps_c = [bank_s[:, 1, :], bank_st[:, 0, :], bank_st[:, 1, :]]
        ps_y, ps_yt, ps_ct = bank_av[:, 0, 0:SEQ], bank_ot[:, 0, 0:SEQ], bank_ot[0:3 * E, 0, SEQ:2 * SEQ]

        x0_in, xr_in, c0_in, cr_in, cst_in, gl_in = (
            sem(n) for n in ("x0_in", "xr_in", "c0_in", "cr_in", "cst_in", "gl_in"))
        small_in, w13_in, w2_in = sem("small_in"), sem("w13_in"), sem("w2_in")
        warm_set = sem("warm_set")
        ones_set = sem("ones_set")
        half_set = sem("half_set")
        values_clear = sem("values_clear")
        consts_set = sem("consts_set")
        gl_done = sem("gl_done")
        tg_ready = sem("tg_ready")
        stat_done = sem("stat_done")
        aggr_done = sem("aggr_done")
        var_ready = sem("var_ready")
        rstd_ready = sem("rstd_ready")
        kin_ready = sem("kin_ready")
        qhat_ready = sem("qhat_ready")
        q_step, k_step = sem("q_step"), sem("k_step")
        pool_passed, dve_passed, pe_passed = sem("pool_passed"), sem("dve_passed"), sem("pe_passed")
        q_built, k_built = sem("q_built"), sem("k_built")
        t_done = sem("t_done")
        qk_ready = sem("qk_ready")
        s_done = sem("s_done")
        max_done = sem("max_done")
        chi_done = sem("chi_done")
        c_ready = sem("c_ready")
        t2_done = sem("t2_done")
        q2_ready = sem("q2_ready")
        st_done = sem("st_done")
        exp_done = sem("exp_done")
        v_ready = sem("v_ready")
        av_done = sem("av_done")
        av_out = sem("av_out")
        ot_done = sem("ot_done")
        recip_done = sem("recip_done")
        o_read = sem("o_read")
        x1_ready = sem("x1_ready")
        stat2_done, aggr2_done, var2_ready = sem("stat2_done"), sem("aggr2_done"), sem("var2_ready")
        rstd2_ready = sem("rstd2_ready")
        wt_done = sem("wt_done")
        gw_hi, gw_ready = sem("gw_hi"), sem("gw_ready")
        w_hi, w_ready = sem("w_hi"), sem("w_ready")
        be2_hi, be2_ready = sem("be2_hi"), sem("be2_ready")
        small_ready = sem("small_ready")
        xh_ready = sem("xh_ready")
        xt_done = sem("xt_done")
        xth_ready = sem("xth_ready")
        xtl_ready = sem("xtl_ready")
        logT_done = sem("logT_done")
        logT_out = sem("logT_out")
        logit_done = sem("logit_done")
        soft_step = sem("soft_step")
        logit_ready, e_ready = sem("logit_ready"), sem("e_ready")
        soft_done = sem("soft_done")
        choose_step = sem("choose_step")
        cc_ready = sem("cc_ready")
        ct_done = sem("ct_done")
        ct_ready = sem("ct_ready")
        h_done = sem("h_done")
        c_done = sem("c_done")
        silu_done = sem("silu_done")
        spread_out = sem("spread_out")
        u_done = sem("u_done")
        hid_done = sem("hid_done")
        w2_done = sem("w2_done")
        y_out = sem("y_out")
        yt_done = sem("yt_done")
        out_ready = sem("out_ready")
        out_sent = sem("out_sent")

        x_v = x.rearrange("(n p) d -> p n d", p=P)
        c_v = ctx_in.rearrange("(n p) d -> p n d", p=P)
        out_v = out.rearrange("(b n p) d -> b p n d", p=P, n=TPB)

        def wait(eng, s, value):
            if not (isinstance(value, int) and value <= 0):
                eng.wait_ge(s, value)

        def back(b, j, steps, per):
            return b + (j - steps) // per, (j - steps) % per

        def exists(b):
            return not isinstance(b, int) or 0 <= b < B

        def batches(eng, body):
            body(0)
            with eng.Fori(0, (B - 2) // 2) as pair:
                body(2 * pair + 1)
                body(2 * pair + 2)
            body(B - 1)
            body(B)

        block = ctx.enter_context(nc.Block())

        @block.sync
        def _(sp):
            sp.dma_start(xs[:, 0:TPB, :], x_v[:, 0:TPB, :]).then_inc(x0_in, 16)
            sp.dma_start(cs[:, 0:TPB, :], c_v[:, 0:TPB, :]).then_inc(c0_in, 16)
            sp.dma_start(xs[:, TPB:TILES, :], x_v[:, TPB:TILES, :]).then_inc(xr_in, 16)
            sp.dma_start(cs[:, TPB:TILES, :], c_v[:, TPB:TILES, :]).then_inc(cr_in, 16)
            sp.dma_start(gwr[:, :], gate_w).then_inc(small_in, 16)
            sp.dma_start(brow[0:RCH, :], be1.rearrange("(c e) i -> c (e i)", e=EPC)).then_inc(small_in, 16)
            sp.dma_start(brow[RCH:CH, :], bs1.rearrange("(a n) -> a n", a=1)).then_inc(small_in, 16)
            sp.dma_start(brow[CH:CH + RCH, :], be3.rearrange("(c e) i -> c (e i)", e=EPC)).then_inc(small_in, 16)
            sp.dma_start(brow[CH + RCH:2 * CH, :], bs3.rearrange("(a n) -> a n", a=1)).then_inc(small_in, 16)
            sp.dma_start(brow[2 * CH:NB1, :], bs2.rearrange("(a n) -> a n", a=1)).then_inc(small_in, 16)
            for part in range(3):
                sp.dma_start(be2f[part * E:(part + 1) * E, :], be2).then_inc(small_in, 16)
            sp.dma_start(spreadf[:, :], spread_in).then_inc(small_in, 16)
            sp.dma_start(w13[:, 0, 0:RCH, :].rearrange("p c (e i) -> p (c e) i", e=EPC),
                         We1.rearrange("e d i -> d e i")).then_inc(w13_in, 16)
            sp.dma_start(w13[:, 1, 0:RCH, :].rearrange("p c (e i) -> p (c e) i", e=EPC),
                         We3.rearrange("e d i -> d e i")).then_inc(w13_in, 16)
            sp.dma_start(w13[:, 0, RCH, :], ws1).then_inc(w13_in, 16)
            sp.dma_start(w13[:, 1, RCH, :], ws3).then_inc(w13_in, 16)
            sp.dma_start(w2[:, 0:RCH, :], We2.rearrange("(c e) i d -> (e i) c d", e=EPC)).then_inc(w2_in, 16)
            sp.dma_start(w2[:, RCH, :], ws2).then_inc(w2_in, 16)
            with sp.Fori(0, B) as b:
                sp.wait_ge(out_ready, b + 1)
                sp.dma_start(out_v[b], outb[:, :, :]).then_inc(out_sent, 16)
            sp.wait_ge(out_sent, 16 * B)

        @block.gpsimd
        def _(pool):
            g = nc.gpsimd

            def parts(b, half, src, rest, cat, places, step, built):
                high, middle, low = places
                v = src[:, half, :, :].rearrange("p n (h d) -> p (n h) d", d=DH)
                rows = cat[:, half, :, :, :].rearrange("p n h r -> p (n h) r")[:, :, 0:QK].rearrange(
                    "p h (c d) -> p h c d", d=DH)

                def at(first, stride, copies):
                    return rows[:, :, first:first + stride * (copies - 1) + 1:stride, :]

                def copy(where, value):
                    return g.tensor_scalar(at(*where), value.unsqueeze(2).to_broadcast(
                        [P, TPB * HPH, where[2], DH]), 1.0, 1.0, ALU.mult, ALU.mult)

                n = 3 * (HALVES * b + half)
                copy(high, v).then_inc(step, 1)
                pool.wait_ge(step, n + 1)
                g.tensor_tensor(rest[:, :, :], v, rows[:, :, high[0], :], ALU.subtract).then_inc(step, 1)
                pool.wait_ge(step, n + 2).then_inc(pool_passed, 1)
                copy(middle, rest[:, :, :]).then_inc(step, 1)
                pool.wait_ge(step, n + 3)
                g.tensor_tensor(rows[:, :, low, :], rest[:, :, :], rows[:, :, middle[0], :],
                                ALU.subtract).then_inc(built, 1)

            def build_q(b, half):
                if not isinstance(b, int) or b > 0:
                    pool.wait_ge(t2_done, UPB * (b - 1) + 2 * half + 2).then_inc(pool_passed, 1)
                pool.wait_ge(qhat_ready, b + 1).then_inc(pool_passed, 1)
                parts(b, half, qhat, qrest, qcat, ((0, 1, 3), (3, 1, 2), 5), q_step, q_built)

            def build_k(b, half):
                if not isinstance(b, int) or b > 0:
                    pool.wait_ge(t_done, UPB * (b - 1) + 2 * half + 2).then_inc(pool_passed, 1)
                pool.wait_ge(kin_ready, b + 1).then_inc(pool_passed, 1)
                parts(b, half, kin, krest, kcat, ((1, 2, 3), (2, 2, 2), 0), k_step, k_built)

            def power(b):
                pool.wait_ge(var_ready, b + 1)
                wait(pool, qhat_ready, b)
                g.tensor_tensor(rstd[:, :], var8[:, :], minus_half[:, 0:TPB], ALU.pow).then_inc(rstd_ready, 1)

            pool.wait_ge(half_set, 1)
            build_k(0, 0)
            power(0)
            build_q(0, 0)
            build_k(0, 1)

            def low_weights(m):
                pool.wait_ge(w_hi, m + 1)
                g.tensor_tensor(w13l[:, m, :, :], w13[:, m, :, :], w13h[:, m, :, :].bitcast(F32),
                                ALU.subtract).then_inc(w_ready, 1)

            def low_biases():
                low = slice(2 * E, 3 * E)
                pool.wait_ge(be2_hi, 1)
                pool.wait_ge(w_ready, 2)
                g.tensor_tensor(be2r[low, :], be2f[low, :], be2r[low, :].bitcast(F32),
                                ALU.subtract).then_inc(be2_ready, 1)
                pool.wait_ge(be2_ready, 1)

            def normalise(b):
                part = slice(TPB * b, TPB * (b + 1))
                pool.wait_ge(var2_ready, b + 1)
                g.tensor_tensor(rstd2[:, part], var2[:, part], minus_half[:, part], ALU.pow).then_inc(rstd2_ready, 1)
                pool.wait_ge(rstd2_ready, b + 1)
                wait(pool, xt_done, b - 1)
                for n in range(TPB):
                    t = TPB * b + n
                    last = g.tensor_scalar(xh[:, b % 2, n, :], xs[:, t, :], mv2[:, t, 0:1], rstd2[:, t:t + 1],
                                           ALU.subtract, ALU.mult)
                last.then_inc(xh_ready, 1)

            def body(b):
                for j in range(UPB):
                    if isinstance(b, int) and b == B - 1:
                        if j == 1:
                            low_weights(0)
                        if j == 2:
                            low_weights(1)
                        if j == 3:
                            low_biases()
                    if j == 0 and exists(b):
                        build_q(b, 1)
                        if exists(b + 1):
                            power(b + 1)
                    if j == 1 and exists(b + 1):
                        build_k(b + 1, 0)
                    if j == 2 and exists(b + 1):
                        build_q(b + 1, 0)
                    if j == 3 and exists(b + 1):
                        build_k(b + 1, 1)

            batches(pool, body)

            for b in range(B):
                normalise(b)

            def experts(b):
                for k in range(RCH):
                    if not exists(b):
                        continue
                    slot = k % SLOTS
                    pool.wait_ge(u_done, CH * b + k + 1)
                    pool.wait_ge(spread_out, RCH * b + k + 1)
                    wait(pool, w2_done, CH * b + k - SLOTS + 1)
                    g.tensor_tensor(hid[:, slot, :], u[:, slot, :], spreadc[:, slot, :], ALU.mult).then_inc(hid_done, 1)

            batches(pool, experts)

        @block.vector
        def _(dve):
            v = nc.vector
            v.memset(warm[:, :], 0.0).then_inc(warm_set, 1)
            v.memset(minus_half[:, :], -0.5).then_inc(half_set, 1)
            v.memset(ones[:, :], 1.0).then_inc(ones_set, 1)

            def tiles(b):
                return bass.ds(TPB * b, TPB)

            def make_kin(b):
                if isinstance(b, int) and b == 0:
                    dve.wait_ge(c0_in, 16)
                if isinstance(b, int) and b == 1:
                    dve.wait_ge(cr_in, 16)
                if not isinstance(b, int) or b > 0:
                    dve.wait_ge(k_built, HALVES * b).then_inc(dve_passed, 1)
                v.tensor_copy(kin[:, :, :, :], cs[:, tiles(b), :].rearrange(
                    "p n (f e) -> p f n e", f=HALVES)).then_inc(kin_ready, 1)

            def make_stats(b):
                if isinstance(b, int) and b == 0:
                    dve.wait_ge(x0_in, 16)
                if isinstance(b, int) and b == 1:
                    dve.wait_ge(xr_in, 16)
                for n in range(TPB):
                    last = v.bn_stats(stats[:, n, :], xs[:, bass.ds(TPB * b + n, 1), :])
                last.then_inc(stat_done, 1)
                dve.wait_ge(stat_done, b + 1).then_inc(dve_passed, 1)
                for n in range(TPB):
                    last = v.bn_aggr(mv[:, n, :], stats[:, n, :])
                last.then_inc(aggr_done, 1)
                dve.wait_ge(aggr_done, b + 1)
                wait(dve, rstd_ready, b)
                v.tensor_scalar(var8[:, :], mv[:, :, 1], EPS, float(DH), ALU.add, ALU.mult).then_inc(var_ready, 1)

            def make_qhat(b):
                dve.wait_ge(rstd_ready, b + 1)
                wait(dve, q_built, HALVES * b)
                for n in range(TPB):
                    last = v.tensor_scalar(qhat[:, :, n, :], xs[:, bass.ds(TPB * b + n, 1), :].rearrange(
                        "p n (f e) -> p (n f) e", f=HALVES), mv[:, n, 0:1], rstd[:, n:n + 1], ALU.subtract, ALU.mult)
                last.then_inc(qhat_ready, 1)

            def make_v(b, half):
                if not isinstance(b, int) or b > 0:
                    dve.wait_ge(av_done, UPB * (b - 1) + 2 * half + 2).then_inc(dve_passed, 1)
                src = cs[:, tiles(b), :].rearrange("p n (f h d) -> p n f h d", f=HALVES, d=DH)
                v.tensor_copy(vcat[:, half, :, :, 0:DH], src[:, :, half, :, :]).then_inc(v_ready, 1)

            def second_q(b, j):
                n = UPB * b + j
                dve.wait_ge(t2_done, n + 1)
                wait(dve, st_done, 2 * n - 2)
                v.tensor_copy(q2T[:, j % 2, :, :], ps_t2).then_inc(q2_ready, 1)

            def maximum(b, j, a):
                dve.wait_ge(s_done, 2 * (UPB * b + j) + a + 1)
                v.tensor_reduce(negmax[:, j % 2, 0, 2 * a:2 * a + 2], bank_s[:, :, 0:P], AX_X, ALU.max, negate=True)
                v.tensor_reduce(negmax[:, j % 2, 1, 2 * a:2 * a + 2], bank_s[:, :, P:3 * P], AX_X, ALU.max,
                                negate=True).then_inc(max_done, 1)

            def shift_rows(j):
                half, first = j // 2, (j % 2) * HPU
                return [qcat[:, half, :, first:first + HPU, R_MAX + part] for part in range(2)]

            def stats_2(b):
                dve.wait_ge(x1_ready, UPB * (b + 1))
                for t in range(TPB * b, TPB * (b + 1)):
                    last = v.bn_stats(stats2[:, t, :], xs[:, t, :])
                last.then_inc(stat2_done, 1)
                dve.wait_ge(stat2_done, b + 1)
                for t in range(TPB * b, TPB * (b + 1)):
                    last = v.bn_aggr(mv2[:, t, :], stats2[:, t, :])
                last.then_inc(aggr2_done, 1)
                dve.wait_ge(aggr2_done, b + 1)
                part = slice(TPB * b, TPB * (b + 1))
                v.tensor_scalar(var2[:, part], mv2[:, part, 1], EPS, None, ALU.add).then_inc(var2_ready, 1)

            def low(b):
                dve.wait_ge(xth_ready, b + 1)
                at = slice(SEQ * b, SEQ * (b + 1))
                v.tensor_tensor(xTl[:, at], ps_xt[b % 2], xTh[:, at].bitcast(F32), ALU.subtract).then_inc(xtl_ready, 1)

            shifted, e_val, p_val, biased = (wide[:, n, :, :] for n in range(4))
            shift, total, inv = (one[:, n, :] for n in range(3))

            def softmax_start(part, first, last):
                n, m = slice(TPB * first, TPB * last), TPB * (last - first)
                dve.wait_ge(logit_done, last)
                v.tensor_reduce(shift[:, n], ps_logit[:, n, :], AX_X, ALU.max, negate=True).then_inc(soft_step, 1)
                dve.wait_ge(soft_step, 4 * part + 1)
                v.tensor_tensor(shifted[:, n, :], ps_logit[:, n, :], shift[:, n].unsqueeze(2).to_broadcast([P, m, E]),
                                ALU.add).then_inc(logit_ready, 1)

            def softmax_end(part, first, last):
                n, m = slice(TPB * first, TPB * last), TPB * (last - first)
                dve.wait_ge(e_ready, part + 1)
                v.tensor_reduce(total[:, n], e_val[:, n, :], AX_X, ALU.add).then_inc(soft_step, 1)
                dve.wait_ge(soft_step, 4 * part + 2)
                v.reciprocal(inv[:, n], total[:, n]).then_inc(soft_step, 1)
                dve.wait_ge(soft_step, 4 * part + 3)
                v.tensor_tensor(p_val[:, n, :], e_val[:, n, :], inv[:, n].unsqueeze(2).to_broadcast([P, m, E]),
                                ALU.mult).then_inc(soft_step, 1)
                dve.wait_ge(soft_step, 4 * part + 4)
                v.tensor_tensor(biased[:, n, :], p_val[:, n, :], gateb[:, :].unsqueeze(1).to_broadcast([P, m, E]),
                                ALU.add).then_inc(soft_done, 1)

            limited, top, numbered, hot1, hot2, weight = (choice[:, n, :, :] for n in range(6))
            per_e, per_g = [P, TPB, E], [P, TPB, GROUPS, GROUPS]
            descending = cst[:, C_E:C_E + E].unsqueeze(1).to_broadcast(per_e)
            lower = cst[:, C_LOWER:C_LOWER + GROUPS * GROUPS].rearrange("p (g o) -> p g o", o=GROUPS).unsqueeze(
                1).to_broadcast(per_g)

            def over_e(value):
                return value.unsqueeze(2).to_broadcast(per_e)

            def choose(b, part):
                past = CHOOSE_STEPS * b
                quads = biased[:, tiles(b), :].rearrange("p n (g c) -> p (n g) c", c=E // GROUPS)
                hi2, lo2 = minmax[:, 0, :, :], minmax[:, 1, :, :]
                top1, mid1, mid2, top2, score, ahead_of, out_of = (narrow[:, n, :] for n in range(7))
                larger, equal, votes = (rank[:, n, :, :, :] for n in range(3))

                if part == 0:
                    v.tensor_tensor(hi2, quads[:, :, 0:2], quads[:, :, 2:4], ALU.max)
                    v.tensor_tensor(lo2, quads[:, :, 0:2], quads[:, :, 2:4], ALU.min).then_inc(choose_step, 1)
                    dve.wait_ge(choose_step, past + 1)
                    v.tensor_tensor(top1, hi2[:, :, 0], hi2[:, :, 1], ALU.max)
                    v.tensor_tensor(mid1, hi2[:, :, 0], hi2[:, :, 1], ALU.min)
                    v.tensor_tensor(mid2, lo2[:, :, 0], lo2[:, :, 1], ALU.max).then_inc(choose_step, 1)
                    dve.wait_ge(choose_step, past + 2)
                    v.tensor_tensor(top2, mid1, mid2, ALU.max).then_inc(choose_step, 1)
                    dve.wait_ge(choose_step, past + 3)
                    v.tensor_tensor(score, top1, top2, ALU.add).then_inc(choose_step, 1)
                if part == 1:
                    gs = score.rearrange("p (n g) -> p n g", g=GROUPS)
                    other, own = gs.unsqueeze(2).to_broadcast(per_g), gs.unsqueeze(3).to_broadcast(per_g)
                    dve.wait_ge(choose_step, past + 4)
                    v.tensor_tensor(larger, other, own, ALU.is_gt)
                    v.tensor_tensor(equal, other, own, ALU.is_equal).then_inc(choose_step, 1)
                    dve.wait_ge(choose_step, past + 5)
                    v.tensor_tensor(votes, equal, lower, ALU.mult).then_inc(choose_step, 1)
                    dve.wait_ge(choose_step, past + 6)
                    v.tensor_tensor(equal, larger, votes, ALU.add).then_inc(choose_step, 1)
                    dve.wait_ge(choose_step, past + 7)
                    v.tensor_reduce(ahead_of.rearrange("p (n g) -> p n g", g=GROUPS), equal, AX_X,
                                    ALU.add).then_inc(choose_step, 1)
                if part == 2:
                    dve.wait_ge(choose_step, past + 8)
                    v.tensor_scalar(out_of, ahead_of, KEEP_GROUPS - 0.5, MASKED, ALU.is_gt,
                                    ALU.mult).then_inc(choose_step, 1)
                    dve.wait_ge(choose_step, past + 9)
                    v.tensor_tensor(limited.rearrange("p n (g c) -> p (n g) c", g=GROUPS), quads, out_of.unsqueeze(
                        2).to_broadcast([P, TPB * GROUPS, E // GROUPS]), ALU.add).then_inc(choose_step, 1)
                    dve.wait_ge(choose_step, past + 10)
                    v.tensor_reduce(best[:, :], limited, AX_X, ALU.max).then_inc(choose_step, 1)
                if part == 3:
                    dve.wait_ge(choose_step, past + 11)
                    v.tensor_tensor(top, limited, over_e(best[:, :]), ALU.is_equal).then_inc(choose_step, 1)
                    dve.wait_ge(choose_step, past + 12)
                    v.tensor_tensor(numbered, top, descending, ALU.mult).then_inc(choose_step, 1)
                    dve.wait_ge(choose_step, past + 13)
                    v.tensor_reduce(first_of[:, :], numbered, AX_X, ALU.max).then_inc(choose_step, 1)
                if part == 4:
                    dve.wait_ge(choose_step, past + 14)
                    v.tensor_tensor(hot1, over_e(first_of[:, :]), descending, ALU.is_equal).then_inc(choose_step, 1)
                    dve.wait_ge(choose_step, past + 15)
                    v.scalar_tensor_tensor(limited, hot1, MASKED, limited, ALU.mult, ALU.add).then_inc(choose_step, 1)
                if part == 5:
                    dve.wait_ge(choose_step, past + 16)
                    v.tensor_reduce(best[:, :], limited, AX_X, ALU.max).then_inc(choose_step, 1)
                    dve.wait_ge(choose_step, past + 17)
                    v.tensor_tensor(top, limited, over_e(best[:, :]), ALU.is_equal).then_inc(choose_step, 1)
                    dve.wait_ge(choose_step, past + 18)
                    v.tensor_tensor(numbered, top, descending, ALU.mult).then_inc(choose_step, 1)
                if part == 6:
                    dve.wait_ge(choose_step, past + 19)
                    v.tensor_reduce(first_of[:, :], numbered, AX_X, ALU.max).then_inc(choose_step, 1)
                    dve.wait_ge(choose_step, past + 20)
                    v.tensor_tensor(hot2, over_e(first_of[:, :]), descending, ALU.is_equal).then_inc(choose_step, 1)
                    dve.wait_ge(choose_step, past + 21)
                    v.tensor_tensor(top, hot1, hot2, ALU.add).then_inc(choose_step, 1)
                if part == 7:
                    dve.wait_ge(choose_step, past + 22)
                    v.tensor_tensor(weight, top, p_val[:, tiles(b), :], ALU.mult).then_inc(choose_step, 1)
                    dve.wait_ge(choose_step, past + 23)
                    v.tensor_copy(c_hi[:, :, :], weight).then_inc(choose_step, 1)
                    dve.wait_ge(choose_step, past + 24)
                    wait(dve, ct_done, b)
                    v.tensor_copy(ccat[:, :, 0:3:2, :], c_hi[:, :, :].bitcast(F32).unsqueeze(2).to_broadcast(
                        [P, TPB, 2, E]))
                    v.tensor_tensor(ccat[:, :, 1, :], weight, c_hi[:, :, :].bitcast(F32), ALU.subtract).then_inc(cc_ready, 1)

            def body(b):
                for j in range(UPB):
                    pb, pj = back(b, j, 1, UPB)
                    ob, oj = back(b, j, 4, UPB)
                    on = UPB * ob + oj
                    o = bank_ot[:, 0, 0:SEQ].rearrange("p (n h w) -> p n h w", n=TPB, w=QUAD)
                    if exists(b):
                        maximum(b, j, 0)
                    if exists(pb):
                        second_q(pb, pj)
                    if j == 0 and exists(b + 1):
                        make_kin(b + 1)
                    if exists(b):
                        maximum(b, j, 1)
                        row_hi, row_lo = shift_rows(j)
                        dve.wait_ge(max_done, 2 * (UPB * b + j) + 2)
                        v.tensor_copy(row_hi, negmax[:, j % 2, :, :]).then_inc(chi_done, 1)
                    if exists(ob):
                        dve.wait_ge(ot_done, on + 1)
                        v.reciprocal(rsum[:, :, :], o[:, :, :, DH]).then_inc(recip_done, 1)
                    if exists(b):
                        dve.wait_ge(chi_done, UPB * b + j + 1)
                        v.tensor_tensor(row_lo, negmax[:, j % 2, :, :], row_hi, ALU.subtract).then_inc(c_ready, 1)
                    if exists(ob):
                        dve.wait_ge(recip_done, on + 1)
                        v.tensor_tensor(onorm[:, :, :].rearrange("p n (h d) -> p n h d", d=DH), o[:, :, :, 0:DH],
                                        rsum[:, :, :].unsqueeze(3).to_broadcast([P, TPB, HPU, DH]),
                                        ALU.mult).then_inc(o_read, 1)
                    if j == 0 and exists(b + 1):
                        make_stats(b + 1)
                    if j == 1 and exists(b + 1):
                        make_qhat(b + 1)
                    if j in (2, 3) and exists(b):
                        make_v(b, j - 2)
                    if exists(ob):
                        dve.wait_ge(o_read, on + 1)
                        columns = slice(oj * HPU * DH, (oj + 1) * HPU * DH)
                        v.scalar_tensor_tensor(xs[:, tiles(ob), columns], onorm[:, :, :], tg[:, 0:1],
                                               xs[:, tiles(ob), columns], ALU.mult, ALU.add).then_inc(x1_ready, 1)
                    if isinstance(b, int) and b == B - 1:
                        stats_2(j)
                    if isinstance(b, int) and b == B:
                        if j == 0:
                            dve.wait_ge(gw_hi, 1)
                            v.tensor_tensor(gwT[:, 1, :], ps_w[:, 0:E], gwT[:, 0, :].bitcast(F32),
                                            ALU.subtract).then_inc(gw_ready, 1)
                            stats_2(4)
                            low(0)
                            stats_2(5)
                        if j == 1:
                            low(1)
                            stats_2(6)
                            low(2)
                        if j == 2:
                            softmax_start(0, 0, 1)
                            low(3)
                            softmax_end(0, 0, 1)
                            dve.wait_ge(soft_done, 1)
                            choose(0, 0)
                            low(4)
                            choose(0, 1)
                        if j == 3:
                            stats_2(B - 1)
                            choose(0, 2)
                            choose(0, 3)
                            low(5)
                            choose(0, 4)
                            choose(0, 5)
                            low(6)
                            choose(0, 6)

            make_stats(0)
            make_kin(0)
            qrows = qcat[:, :, :, :, :].rearrange("p f n h r -> p (f n h) r")
            krows = kcat[:, :, :, :, :].rearrange("p f n h r -> p (f n h) r")
            v.memset(qrows[:, :, R_MAX:ROWS], 0.0)
            v.memset(krows[:, :, R_MAX:K_ST], 1.0)
            v.memset(krows[:, :, K_ST:ROWS], 0.0)
            dve.wait_ge(cst_in, 16)
            for half in range(HALVES):
                slopes = cst[:, C_SLOPE + half * 3 * HPH:C_SLOPE + (half + 1) * 3 * HPH].rearrange(
                    "p (h c) -> p h c", c=3)
                for n in range(TPB):
                    v.tensor_copy(qcat[:, half, n, :, R_SLOPE:R_MAX], slopes)
            for n in range(TPB):
                last = v.tensor_copy(kcat[:, :, n, :, R_SLOPE:R_MAX],
                                     cst[:, C_POS + n:C_POS + n + 1].unsqueeze(2).unsqueeze(3).to_broadcast(
                                         [P, HALVES, HPH, 3]))
            v.tensor_copy(identb[:, :], ident)
            v.tensor_copy(maskb[:, :], cst[:, C_MASK:C_MASK + P]).then_inc(consts_set, 1)
            make_qhat(0)
            v.memset(vcat[:, :, :, :, :], 0.0).then_inc(values_clear, 1)
            dve.wait_ge(values_clear, 1)
            v.memset(vcat[:, :, :, :, DH].rearrange("p f n h -> p (f n) h"), 1.0)
            dve.wait_ge(tg_ready, 1)
            batches(dve, body)

            low(B - 1)
            choose(0, 7)
            dve.wait_ge(soft_done, 1)
            softmax_start(1, 1, B)
            softmax_end(1, 1, B)
            dve.wait_ge(soft_done, 2)

            dve.wait_ge(small_ready, 1)
            def experts(b):
                for k in range(CH):
                    pb = b - 1
                    if k == 4 and exists(pb):
                        dve.wait_ge(yt_done, pb + 1)
                        v.scalar_tensor_tensor(outb[:, :, :], ps_yt.rearrange("p (n d) -> p n d", n=TPB), tg[:, 1:2],
                                               xs[:, tiles(pb), :], ALU.mult, ALU.add).then_inc(out_ready, 1)
                    if not exists(b):
                        continue
                    if k == RCH and exists(pb):
                        dve.wait_ge(out_sent, 16 * (pb + 1))
                    c = CH * b + k
                    dve.wait_ge(silu_done, c + 1)
                    ub, uk = back(b, k, SLOTS, CH)
                    wait(dve, hid_done, RCH * ub + min(uk + 1, RCH))
                    target = u
                    if k == RCH:
                        target = hid
                        wait(dve, w2_done, c - SLOTS + 1)
                    v.scalar_tensor_tensor(target[:, k % SLOTS, :], ps_h[k % SLOTS][:, SEQ:2 * SEQ],
                                           bcol[:, CH + k:CH + k + 1], s1[:, k % SLOTS, :],
                                           ALU.add, ALU.mult).then_inc(u_done, 1)
                    if exists(b + 1) and k < RCH:
                        choose(b + 1, k)

            batches(dve, experts)

        @block.scalar
        def _(act):
            s = nc.scalar
            act.dma_start(cst[:, :], const_in).then_inc(cst_in, 16)
            act.dma_start(gl[:, 0:1], g_xattn.rearrange("(a n) -> a n", a=1)).then_inc(gl_in, 16)
            act.dma_start(gl[:, 1:2], g_ffn.rearrange("(a n) -> a n", a=1)).then_inc(gl_in, 16)
            act.dma_start(gl[:, 2:2 + E], gate_b.rearrange("(a n) -> a n", a=1)).then_inc(gl_in, 16)
            act.wait_ge(gl_done, 1)
            s.activation(tg[:, :], bank_ot[:, 0, 0:2], ACT.Tanh)
            s.copy(gateb[:, :], bank_ot[:, 0, 2:2 + E]).then_inc(tg_ready, 1)

            def operands(b, j):
                n = UPB * b + j
                act.wait_ge(t_done, n + 1)
                wait(act, st_done, 2 * (n - UPB) + 2)
                s.copy(qkT[:, j, :, :], ps_t).then_inc(qk_ready, 1)

            def exponent(b, j, a):
                n = UPB * b + j
                act.wait_ge(st_done, 2 * n + a + 1)
                wait(act, av_done, n - 1)
                s.activation(prob[:, j % 2, 2 * a:2 * a + 2, :], bank_st[:, :, 0:3 * P], ACT.Exp).then_inc(exp_done, 1)

            def outputs(b, j):
                n = UPB * b + j
                act.wait_ge(av_done, n + 1)
                wait(act, ot_done, n - 1)
                s.copy(avT[:, j % 2, :], bank_av[:, 0, 0:SEQ]).then_inc(av_out, 1)

            def high(b):
                act.wait_ge(xt_done, b + 1)
                s.copy(xTh[:, SEQ * b:SEQ * (b + 1)], ps_xt[b % 2]).then_inc(xth_ready, 1)

            def log_out(b):
                act.wait_ge(logT_done, b + 1)
                wait(act, logit_done, b - 1)
                s.copy(logT[:, b % 2, :], ps_logT).then_inc(logT_out, 1)

            def softmax_exp(part, first, last):
                act.wait_ge(logit_ready, part + 1)
                n = slice(TPB * first, TPB * last)
                s.activation(wide[:, 1, n, :], wide[:, 0, n, :], ACT.Exp).then_inc(e_ready, 1)

            operands(0, 0)

            def body(b):
                for j in range(UPB):
                    nb, nj = back(b, j, -1, UPB)
                    eb, ej = back(b, j, 2, UPB)
                    ab, aj = back(b, j, 3, UPB)
                    if exists(eb):
                        exponent(eb, ej, 0)
                    if exists(b) and exists(nb):
                        operands(nb, nj)
                    if exists(eb):
                        exponent(eb, ej, 1)
                    if exists(ab):
                        outputs(ab, aj)
                    if isinstance(b, int) and b == B - 1:
                        if j == 0:
                            act.wait_ge(w13_in, 16 * 4)
                            s.copy(w13h[:, 0, :, :], w13[:, 0, :, :]).then_inc(w_hi, 1)
                        if j == 1:
                            s.copy(w13h[:, 1, :, :], w13[:, 1, :, :]).then_inc(w_hi, 1)
                        if j == 2:
                            act.wait_ge(small_in, 16 * 10)
                            s.copy(be2r[:, :], be2f[:, :]).then_inc(be2_hi, 1)
                            s.copy(spreadr[:, :], spreadf[:, :]).then_inc(small_ready, 1)
                    if isinstance(b, int) and b == B:
                        if j == 0:
                            act.wait_ge(wt_done, 1)
                            s.copy(bcol[:, :], ps_w[:, E:E + NB1])
                            s.copy(gwT[:, 0, :], ps_w[:, 0:E]).then_inc(gw_hi, 1)
                            high(0)
                        if j == 1:
                            high(1)
                            log_out(0)
                            high(2)
                            log_out(1)
                        if j == 2:
                            high(3)
                            softmax_exp(0, 0, 1)
                            log_out(2)
                            high(4)
                            log_out(3)
                        if j == 3:
                            high(5)
                            log_out(4)
                            high(6)
                            log_out(5)

            batches(act, body)

            high(B - 1)
            log_out(B - 2)
            log_out(B - 1)
            softmax_exp(1, 1, B)

            def weights_out(b):
                act.wait_ge(ct_done, b + 1)
                s.copy(cT[:, bass.ds(SEQ * b, SEQ)], ps_ct).then_inc(ct_ready, 1)

            weights_out(0)

            def experts(b):
                for k in range(CH):
                    if k == 2 and exists(b - 1):
                        act.wait_ge(w2_done, CH * b)
                        s.activation(yT[:, :], ps_y, ACT.Identity, bias=bcol[:, 2 * CH:NB1]).then_inc(y_out, 1)
                    if not exists(b):
                        continue
                    c, slot = CH * b + k, k % SLOTS
                    act.wait_ge(h_done, c + 1)
                    wait(act, u_done, c - SLOTS + 1)
                    s.activation(s1[:, slot, :], ps_h[slot][:, 0:SEQ], ACT.Silu,
                                 bias=bcol[:, k:k + 1]).then_inc(silu_done, 1)
                    if k < RCH:
                        cb, ck = back(b, k, SLOTS, CH)
                        act.wait_ge(c_done, RCH * b + k + 1)
                        wait(act, hid_done, RCH * cb + min(ck + 1, RCH))
                        s.copy(spreadc[:, slot, :], ps_c[slot][:, 0:SEQ]).then_inc(spread_out, 1)
                    elif exists(b + 1):
                        weights_out(b + 1)

            batches(act, experts)

        @block.tensor
        def _(pe):
            mm, transpose = nc.tensor.matmul, nc.tensor.transpose
            mask = maskb[:, :].unsqueeze(1).to_broadcast([P, 2, P])
            eye = identb[:, :].unsqueeze(1).to_broadcast([P, 2, P])

            def transposed(b, j):
                n, half, first = UPB * b + j, j // 2, (j % 2) * HPU
                pe.wait_ge(q_built, HALVES * b + half + 1)
                pe.wait_ge(k_built, HALVES * b + half + 1)
                wait(pe, qk_ready, n)
                for a in range(2):
                    for which, cat in enumerate((qcat, kcat)):
                        for t in range(TPB):
                            at = (which * TPB + t) * P
                            last = transpose(ps_t[:, a, at:at + P], cat[:, half, t, first + 2 * a:first + 2 * a + 2, :]
                                             .rearrange("p h r -> p (h r)"), identb[:, :])
                last.then_inc(t_done, 1)

            def scores(b, j, a):
                n = UPB * b + j
                pe.wait_ge(qk_ready, n + 1)
                wait(pe, max_done, 2 * n + a)
                for p in range(2):
                    rows = slice(p * ROWS, p * ROWS + K_S)
                    q, k = qkT[rows, j, a, 0:SEQ], qkT[rows, j, a, SEQ:2 * SEQ]
                    diagonal = bank_s[:, p, 0:3 * P].rearrange("p (x n) -> p x n", n=P)[:, 0:3:2, :]
                    mm(diagonal, identb[:, :], mask, start=True, stop=False, skip_group_check=True)
                    mm(bank_s[:, p, 0:P], q[:, 0:P], k[:, 0:P], start=False, stop=True, skip_group_check=True)
                    last = mm(bank_s[:, p, P:3 * P], q[:, P:SEQ], k, start=False, stop=True, skip_group_check=True)
                last.then_inc(s_done, 1)

            def second(b, j):
                n, half, first = UPB * b + j, j // 2, (j % 2) * HPU
                pe.wait_ge(c_ready, n + 1)
                wait(pe, q2_ready, n)
                for a in range(2):
                    for t in range(TPB):
                        last = transpose(ps_t2[:, a, t * P:(t + 1) * P], qcat[:, half, t, first + 2 * a:first + 2 * a + 2, :]
                                         .rearrange("p h r -> p (h r)"), identb[:, :])
                last.then_inc(t2_done, 1)

            def scores_t(b, j, a):
                n = UPB * b + j
                pe.wait_ge(q2_ready, n + 1)
                wait(pe, exp_done, 2 * n + a)
                for p in range(2):
                    rows = slice(p * ROWS, p * ROWS + K_ST)
                    k = qkT[rows, j, a, SEQ:2 * SEQ]
                    diagonal = bank_st[:, p, 0:3 * P].rearrange("p (x n) -> p x n", n=P)[:, 0:3:2, :]
                    mm(diagonal, maskb[:, :], eye, start=True, stop=False, skip_group_check=True)
                    mm(bank_st[:, p, 0:SEQ], k[:, 0:P], q2T[rows, j % 2, a, :], start=False, stop=True, skip_group_check=True)
                    last = mm(bank_st[:, p, SEQ:3 * P], k[:, P:SEQ], q2T[rows, j % 2, a, P:SEQ], start=False, stop=True,
                              skip_group_check=True)
                last.then_inc(st_done, 1)

            def values(b, j):
                n, half, first = UPB * b + j, j // 2, (j % 2) * HPU
                pe.wait_ge(exp_done, 2 * n + 2)
                pe.wait_ge(v_ready, HALVES * b + half + 1)
                wait(pe, av_out, n)
                for h in range(HPU):
                    mm(bank_av[h * QUAD:(h + 1) * QUAD, 0, 0:SEQ], vcat[:, half, 0, first + h, :],
                       prob[:, j % 2, h, 0:SEQ], start=True, stop=False, skip_group_check=True,
                       tile_position=(0, h * QUAD))
                for h in range(HPU):
                    last = mm(bank_av[h * QUAD:(h + 1) * QUAD, 0, P:SEQ], vcat[:, half, 1, first + h, :],
                              prob[:, j % 2, h, SEQ:3 * P], start=False, stop=True, skip_group_check=True,
                              tile_position=(0, h * QUAD))
                last.then_inc(av_done, 1)

            def outputs(b, j):
                n = UPB * b + j
                pe.wait_ge(av_out, n + 1)
                wait(pe, o_read, n)
                for t in range(TPB):
                    last = transpose(bank_ot[:, 0, t * P:(t + 1) * P], avT[:, j % 2, t * P:(t + 1) * P], ident)
                last.then_inc(ot_done, 1)

            def small_transposes():
                pe.wait_ge(small_in, 16 * 10)
                pe.wait_ge(max_done, 2 * UNITS)
                transpose(ps_w[:, 0:E], gwr[:, :], ident[0:E, 0:E])
                transpose(ps_w[:, E:E + NB1], brow[:, :], ident[0:NB1, 0:NB1]).then_inc(wt_done, 1)

            def tokens_t(b):
                pe.wait_ge(xh_ready, b + 1)
                wait(pe, xtl_ready, b - 1)
                for n in range(TPB):
                    last = transpose(ps_xt[b % 2][:, n * P:(n + 1) * P], xh[:, b % 2, n, :], ident)
                last.then_inc(xt_done, 1)

            def logits(b):
                pe.wait_ge(gw_ready, 1)
                pe.wait_ge(xtl_ready, b + 1)
                wait(pe, logT_out, b)
                at = slice(SEQ * b, SEQ * (b + 1))
                mm(ps_logT, gwT[:, 0, :], xTh[:, at], start=True, stop=False)
                mm(ps_logT, gwT[:, 1, :], xTh[:, at], start=False, stop=False)
                mm(ps_logT, gwT[:, 0, :], xTl[:, at], start=False, stop=True).then_inc(logT_done, 1)

            def by_token(b):
                pe.wait_ge(logT_out, b + 1)
                if b == 1:
                    pe.wait_ge(logit_ready, 1)
                for n in range(TPB):
                    last = transpose(ps_logit[:, TPB * b + n, :], logT[:, b % 2, n * P:(n + 1) * P], ident[0:E, 0:E])
                last.then_inc(logit_done, 1)

            def keep_warm(products):
                for _ in range(products):
                    mm(bank_av[:, 0, :], warm[:, 0:P], warm[:, :], start=True, stop=True)

            pe.wait_ge(warm_set, 1)
            keep_warm(WARM_UP)

            pe.wait_ge(ones_set, 1)
            pe.wait_ge(gl_in, 16 * 3)
            mm(bank_ot[:, 0, 0:2 + E], ones[:, :], gl[:, :], start=True, stop=True).then_inc(gl_done, 1)
            pe.wait_ge(consts_set, 1)
            transposed(0, 0)
            keep_warm(4)

            def body(b):
                for j in range(UPB):
                    nb, nj = back(b, j, -1, UPB)
                    pb, pj = back(b, j, 1, UPB)
                    ab, aj = back(b, j, 3, UPB)
                    ob, oj = back(b, j, 4, UPB)
                    eb, ej = back(b, j, 2, UPB)
                    if exists(b):
                        scores(b, j, 0)
                    if exists(pb):
                        second(pb, pj)
                    if exists(eb):
                        scores_t(eb, ej, 0)
                    if exists(b) and exists(nb):
                        transposed(nb, nj)
                    if isinstance(b, int) and b == 0 and j < 3:
                        keep_warm(3)
                    if exists(ob):
                        if isinstance(ob, int) and ob == 0:
                            pe.wait_ge(tg_ready, 1)
                        outputs(ob, oj)
                    if exists(b):
                        scores(b, j, 1)
                    if isinstance(b, int) and b == 0 and j < 2:
                        keep_warm(5)
                    if exists(eb):
                        scores_t(eb, ej, 1)
                    if exists(ab):
                        values(ab, aj)
                    if isinstance(b, int) and b == B:
                        if j == 0:
                            small_transposes()
                            tokens_t(0)
                        if j == 1:
                            tokens_t(1)
                            logits(0)
                            tokens_t(2)
                            logits(1)
                            by_token(0)
                        if j == 2:
                            tokens_t(3)
                            logits(2)
                            by_token(1)
                            tokens_t(4)
                            logits(3)
                            by_token(2)
                        if j == 3:
                            tokens_t(5)
                            logits(4)
                            by_token(3)
                            tokens_t(6)
                            logits(5)
                            by_token(4)

            batches(pe, body)

            tokens_t(B - 1)
            logits(B - 2)
            by_token(B - 3)
            logits(B - 1)
            by_token(B - 2)
            by_token(B - 1)

            pe.wait_ge(w_ready, 2)
            pe.wait_ge(be2_ready, 1)
            pe.wait_ge(small_ready, 1)
            pe.wait_ge(w2_in, 16 * 2)

            def weights_t(b):
                pe.wait_ge(cc_ready, b + 1).then_inc(pe_passed, 1)
                for n in range(TPB):
                    last = transpose(ps_ct[:, n * P:(n + 1) * P], ccat[:, n, :, :].rearrange("p c e -> p (c e)"), ident)
                last.then_inc(ct_done, 1)

            def hidden(b, k):
                slot, tokens = k % SLOTS, bass.ds(SEQ * b, SEQ)
                cb, ck = back(b, k, SLOTS, CH)
                wait(pe, spread_out, RCH * cb + min(ck + 1, RCH))
                wait(pe, u_done, CH * b + k - SLOTS + 1)
                for m in range(2):
                    target = ps_h[slot][:, m * SEQ:(m + 1) * SEQ]
                    mm(target, w13h[:, m, k, :], xTh[:, tokens], start=True, stop=False, skip_group_check=True)
                    mm(target, w13h[:, m, k, :], xTl[:, tokens], start=False, stop=False, skip_group_check=True)
                    last = mm(target, w13l[:, m, k, :], xTh[:, tokens], start=False, stop=True, skip_group_check=True)
                last.then_inc(h_done, 1)
                if isinstance(b, int) and b == 0 and k == 0:
                    weights_t(0)
                    pe.wait_ge(logit_ready, 2)
                if k == 0:
                    pe.wait_ge(ct_ready, b + 1).then_inc(pe_passed, 1)
                if k < RCH:
                    mm(ps_c[slot][:, 0:SEQ], spreadr[:, k * P:(k + 1) * P], cT[0:2 * E, tokens],
                       start=True, stop=True).then_inc(c_done, 1)

            def down(b, k):
                if k == 0:
                    wait(pe, y_out, b)
                if k < RCH:
                    pe.wait_ge(hid_done, RCH * b + k + 1)
                else:
                    pe.wait_ge(u_done, CH * b + k + 1)
                last = mm(ps_y, w2[:, k, :], hid[:, k % SLOTS, :], start=k == 0, stop=k == RCH, skip_group_check=True)
                if k == 0:
                    last = mm(ps_y, be2r[:, :], cT[:, bass.ds(SEQ * b, SEQ)], start=False, stop=False,
                              skip_group_check=True)
                last.then_inc(w2_done, 1)

            def experts(b):
                for k in range(CH):
                    if exists(b):
                        hidden(b, k)
                    db, dk = back(b, k, 2, CH)
                    if k == 3 and exists(b - 1):
                        pe.wait_ge(y_out, b)
                        for n in range(TPB):
                            last = transpose(ps_yt[:, n * P:(n + 1) * P], yT[:, n * P:(n + 1) * P], ident)
                        last.then_inc(yt_done, 1)
                    if exists(db):
                        down(db, dk)
                    if k == CH - 1 and exists(b) and exists(b + 1):
                        weights_t(b + 1)

            batches(pe, experts)


def kernel(**inputs):
    import numpy as np
    import concourse.bacc as bacc
    from concourse import mybir
    from concourse.bass_utils import run_bass_kernel_spmd
    nc = bacc.Bacc("TRN2", target_bir_lowering=False, num_devices=1)
    table, spread = constants()
    arrays = {"x": np.ascontiguousarray(inputs["x"]).reshape(B * SEQ, D),
              "ctx": np.ascontiguousarray(inputs["ctx_1024"]).reshape(B * SEQ, D),
              "g_xattn": np.ascontiguousarray(inputs["g_xattn"]),
              "g_ffn": np.ascontiguousarray(inputs["g_ffn"])}
    for name in ("gate_w", "gate_b", "We1", "be1", "We2", "be2", "We3", "be3", "ws1", "bs1", "ws2", "bs2", "ws3", "bs3"):
        arrays[name] = np.ascontiguousarray(inputs["L0_ffn_" + name])
    arrays["table"], arrays["spread"] = table, spread
    ins = [nc.dram_tensor(name + "_in", a.shape, mybir.dt.float32, kind="ExternalInput").ap()
           for name, a in arrays.items()]
    out = nc.dram_tensor("y_out", (B * SEQ, D), mybir.dt.float32, kind="ExternalOutput").ap()
    program(nc, *ins, out)
    res = run_bass_kernel_spmd(nc, [{name + "_in": a for name, a in arrays.items()}], core_ids=[0])
    return res.results[0]["y_out"].reshape(B, SEQ, D)
```

```python
from contextlib import ExitStack

import numpy as np

import concourse.bass as bass
from concourse import mybir

F32 = mybir.dt.float32
F32R = mybir.dt.float32r
BF16 = mybir.dt.bfloat16
ALU = mybir.AluOpType
ACT = mybir.ActivationFunctionType
AX_X = mybir.AxisListType.X

P = 128
B, SEQ, D = 8, 256, 128
TPB = SEQ // P
TILES = B * TPB
H = 16
DH = D // H
UPB = 4
HPU = H // UPB
HALVES = 2
HPH = H // HALVES
QUAD = 32
BANK = 512
UNITS = B * UPB
EPS = 1e-5
MASKED = -1e30

ROWS = 64
QK = 6 * DH
R_SLOPE = QK
R_MAX = QK + 3
K_S = QK + 3
K_ST = QK + 5

E, GROUPS, TOPK = 16, 4, 2
INTER = 64
EPC = P // INTER
RCH = E // EPC
CH = RCH + 1
KEEP_GROUPS = 2
CHOOSE_PARTS = 7
CHOOSE_STEPS = 19
ROUTED = ((0, 2), (2, 4), (4, 6), (6, 7), (7, 8))
SHARES = ((0, 1), (1, 7), (7, 8))
STAT_GROUPS = ((0, 1), (1, 2), (2, 3), (3, 4), (4, 6), (6, 7), (7, 8))
WARM_UP = 20
SLOTS = 3
NB1 = 2 * CH + 1

C_ID, C_MASK, C_SLOPE, C_POS, C_E, C_LOWER = 0, P, 2 * P, 2 * P + 3 * H, 2 * P + 3 * H + TPB, 2 * P + 3 * H + TPB + E
C_END = C_LOWER + GROUPS * GROUPS


def to_bfloat16(v):
    bits = v.view(np.uint32)
    return ((bits + 0x7FFF + ((bits >> 16) & 1)) & np.uint32(0xFFFF0000)).view(np.float32)


def constants():
    c = np.zeros((P, C_END), np.float32)
    c[:, C_ID:C_ID + P] = np.eye(P)
    t, s = np.arange(P)[:, None], np.arange(P)[None, :]
    c[:, C_MASK:C_MASK + P] = np.where(s > t, MASKED, 0.0)
    rest = np.cumprod(np.full((H,), 2.0 ** (-8.0 / H), np.float32), dtype=np.float32)
    for part in range(3):
        piece = to_bfloat16(rest)
        c[:, C_SLOPE + part:C_SLOPE + 3 * H:3] = piece
        rest = rest - piece
    for n in range(TPB):
        c[:, C_POS + n] = np.arange(P) + n * P
    c[:, C_E:C_E + E] = E - np.arange(E)
    c[:, C_LOWER:C_END] = (np.tril(np.ones((GROUPS, GROUPS)), -1)
                           - (KEEP_GROUPS - 0.5) * np.eye(GROUPS)).reshape(-1)
    spread = np.zeros((2 * E, RCH, P), np.float32)
    for e in range(E):
        spread[e, e // EPC, (e % EPC) * INTER:(e % EPC + 1) * INTER] = 1.0
        spread[E + e] = spread[e]
    return c, spread.reshape(2 * E, RCH * P)


def program(nc, x, ctx_in, g_xattn, g_ffn, gate_w, gate_b, We1, be1, We2, be2, We3, be3,
            ws1, bs1, ws2, bs2, ws3, bs3, const_in, spread_in, out):
    ctx = ExitStack()
    with ctx:
        def sb(name, shape, dt=F32):
            return ctx.enter_context(nc.sbuf_tensor(name, shape, dt))

        def sem(name):
            return ctx.enter_context(nc.semaphore(name))

        cst = sb("cst", [P, C_END])
        ident = cst[:, C_ID:C_ID + P]
        identb = sb("identb", [P, P], BF16)
        warm = sb("warm", [P, BANK], BF16)
        maskb = sb("maskb", [P, P], BF16)
        xs = sb("xs", [P, TILES, D])
        cs = sb("cs", [P, TILES, D])
        stats = sb("stats", [P, TPB, 6])
        mv = sb("mv", [P, TPB, 2])
        var8 = sb("var8", [P, TPB])
        minus_half = sb("minus_half", [P, TILES])
        rstd = sb("rstd", [P, TPB])
        qhat = sb("qhat", [P, HALVES, TPB, D // HALVES])
        kin = sb("kin", [P, HALVES, TPB, D // HALVES])
        qrest = sb("qrest", [P, TPB * HPH, DH])
        krest = sb("krest", [P, TPB * HPH, DH])
        qcat = sb("qcat", [P, HALVES, TPB, HPH, ROWS], BF16)
        kcat = sb("kcat", [P, HALVES, TPB, HPH, ROWS], BF16)
        vcat = sb("vcat", [P, HALVES, TPB, HPH, QUAD])
        qkT = sb("qkT", [P, UPB, 2, 2 * SEQ], BF16)
        q2T = sb("q2T", [P, 2, 2, SEQ], BF16)
        negmax = sb("negmax", [P, 2, TPB, HPU])
        prob = sb("prob", [P, 2, HPU, 3 * P])
        avT = sb("avT", [P, 2, SEQ])
        rsum = sb("rsum", [P, TPB, HPU])
        onorm = sb("onorm", [P, TPB, HPU * DH])
        gl = sb("gl", [1, 2 + E])
        ones = sb("ones", [1, P])
        tg = sb("tg", [P, 2])
        gateb = sb("gateb", [P, E])
        gwr = sb("gwr", [E, D])
        gwT = sb("gwT", [P, 2, E], F32R)
        brow = sb("brow", [NB1, P])
        bcol = sb("bcol", [P, NB1])
        w13 = sb("w13", [P, 2, CH, P])
        w13h = sb("w13h", [P, 2, CH, P], F32R)
        w13l = sb("w13l", [P, 2, CH, P], F32R)
        w2 = sb("w2", [P, CH, D])
        be2f = sb("be2f", [3 * E, D])
        be2r = sb("be2r", [3 * E, D], F32R)
        spreadf = sb("spreadf", [2 * E, RCH * P])
        spreadr = sb("spreadr", [2 * E, RCH * P], F32R)
        stats2 = sb("stats2", [P, TILES, 6])
        mv2 = sb("mv2", [P, TILES, 2])
        centred = sb("centred", [P, TPB, D])
        var2 = sb("var2", [P, TILES])
        rstd2 = sb("rstd2", [P, TILES])
        xh = sb("xh", [P, TILES, D])
        xTh = sb("xTh", [P, B * SEQ], F32R)
        xTl = sb("xTl", [P, B * SEQ], F32R)
        logT = sb("logT", [E, 2, 2 * SEQ])
        wide = sb("wide", [P, 4, TILES, E])
        one = sb("one", [P, 3, TILES])
        choice = sb("choice", [P, 6, TPB, E])
        narrow = sb("narrow", [P, 7, TPB * GROUPS])
        minmax = sb("minmax", [P, 2, TPB * GROUPS, 2])
        equal = sb("equal", [P, TPB * GROUPS, GROUPS])
        rank = sb("rank", [P, TPB * GROUPS, 2, GROUPS])
        best = sb("best", [P, TPB])
        first_of = sb("first_of", [P, TPB])
        ccat = sb("ccat", [P, TPB, 3, E], F32R)
        cT = sb("cT", [3 * E, B * SEQ], F32R)
        s1 = sb("s1", [P, SLOTS, SEQ])
        spreadc = sb("spreadc", [P, SLOTS, SEQ])
        u = sb("u", [P, SLOTS, SEQ])
        hid = sb("hid", [P, SLOTS, SEQ])
        yT = sb("yT", [P, SEQ])
        outb = sb("outb", [P, TPB, D])

        def psum(name, banks=1):
            return ctx.enter_context(nc.psum_tensor(name, [P, banks, BANK], F32))

        bank_t, bank_t2, bank_s, bank_st, bank_av, bank_ot = (
            psum("bank_t"), psum("bank_t2"), psum("bank_s", 2), psum("bank_st", 2), psum("bank_av"), psum("bank_ot"))
        ps_t = bank_t[:, 0, :].bitcast(BF16).rearrange("p (a n) -> p a n", a=2)
        ps_t2 = bank_t2[:, 0, 0:SEQ].bitcast(BF16).rearrange("p (a n) -> p a n", a=2)
        ps_xt = [bank_t[:, 0, :], bank_t2[:, 0, :]]
        ps_logT = bank_s[0:E, 0, :]
        ps_logit = bank_s[:, 1, 0:TILES * E].rearrange("p (n e) -> p n e", e=E)
        ps_w = bank_s[:, 1, TILES * E:]
        ps_h = [bank_t[:, 0, :], bank_t2[:, 0, :], bank_s[:, 0, :]]
        ps_c = [bank_s[:, 1, :], bank_st[:, 0, :], bank_st[:, 1, :]]
        ps_y, ps_yt, ps_ct = bank_av[:, 0, 0:SEQ], bank_ot[:, 0, 0:SEQ], bank_ot[0:3 * E, 0, SEQ:2 * SEQ]

        x0_in, xr_in, c0_in, cr_in, cst_in, gl_in = (
            sem(n) for n in ("x0_in", "xr_in", "c0_in", "cr_in", "cst_in", "gl_in"))
        small_in, w13_in, w2_in = sem("small_in"), sem("w13_in"), sem("w2_in")
        warm_set = sem("warm_set")
        ones_set = sem("ones_set")
        half_set = sem("half_set")
        values_clear = sem("values_clear")
        consts_set = sem("consts_set")
        gl_done = sem("gl_done")
        tg_ready = sem("tg_ready")
        stat_done = sem("stat_done")
        aggr_done = sem("aggr_done")
        var_ready = sem("var_ready")
        rstd_ready = sem("rstd_ready")
        kin_ready = sem("kin_ready")
        qhat_ready = sem("qhat_ready")
        q_step, k_step = sem("q_step"), sem("k_step")
        pool_passed, dve_passed, pe_passed = sem("pool_passed"), sem("dve_passed"), sem("pe_passed")
        q_built, k_built = sem("q_built"), sem("k_built")
        t_done = sem("t_done")
        qk_ready = sem("qk_ready")
        s_done = sem("s_done")
        max_done = sem("max_done")
        chi_done = sem("chi_done")
        c_ready = sem("c_ready")
        t2_done = sem("t2_done")
        q2_ready = sem("q2_ready")
        st_done = sem("st_done")
        exp_done = sem("exp_done")
        v_ready = sem("v_ready")
        av_done = sem("av_done")
        av_out = sem("av_out")
        ot_done = sem("ot_done")
        recip_done = sem("recip_done")
        o_read = sem("o_read")
        x1_ready = sem("x1_ready")
        stat2_done, aggr2_done, var2_ready = sem("stat2_done"), sem("aggr2_done"), sem("var2_ready")
        rstd2_ready = sem("rstd2_ready")
        centred_done = sem("centred_done")
        wt_done = sem("wt_done")
        gw_hi, gw_ready = sem("gw_hi"), sem("gw_ready")
        w_hi, w_ready = sem("w_hi"), sem("w_ready")
        be2_hi, be2_ready = sem("be2_hi"), sem("be2_ready")
        small_ready = sem("small_ready")
        xh_ready = sem("xh_ready")
        xt_done = sem("xt_done")
        xth_ready = sem("xth_ready")
        xtl_ready = sem("xtl_ready")
        logT_done = sem("logT_done")
        logT_out = sem("logT_out")
        logit_done = sem("logit_done")
        soft_step = sem("soft_step")
        logit_ready, e_ready = sem("logit_ready"), sem("e_ready")
        soft_done = sem("soft_done")
        choose_step = sem("choose_step")
        cc_ready = sem("cc_ready")
        ct_done = sem("ct_done")
        ct_ready = sem("ct_ready")
        h_done = sem("h_done")
        c_done = sem("c_done")
        silu_done = sem("silu_done")
        spread_out = sem("spread_out")
        u_done = sem("u_done")
        hid_done = sem("hid_done")
        w2_done = sem("w2_done")
        y_out = sem("y_out")
        yt_done = sem("yt_done")
        out_ready = sem("out_ready")
        out_sent = sem("out_sent")

        x_v = x.rearrange("(n p) d -> p n d", p=P)
        c_v = ctx_in.rearrange("(n p) d -> p n d", p=P)
        out_v = out.rearrange("(b n p) d -> b p n d", p=P, n=TPB)

        def wait(eng, s, value):
            if not (isinstance(value, int) and value <= 0):
                eng.wait_ge(s, value)

        def back(b, j, steps, per):
            return b + (j - steps) // per, (j - steps) % per

        def routed(group):
            first, last = ROUTED[group]
            return slice(SEQ * first, SEQ * last), slice(0, SEQ * (last - first))

        def exists(b):
            return not isinstance(b, int) or 0 <= b < B

        def batches(eng, body):
            body(0)
            with eng.Fori(0, (B - 2) // 2) as pair:
                body(2 * pair + 1)
                body(2 * pair + 2)
            body(B - 1)
            body(B)

        block = ctx.enter_context(nc.Block())

        @block.sync
        def _(sp):
            sp.dma_start(xs[:, 0:TPB, :], x_v[:, 0:TPB, :]).then_inc(x0_in, 16)
            sp.dma_start(cs[:, 0:TPB, :], c_v[:, 0:TPB, :]).then_inc(c0_in, 16)
            sp.dma_start(xs[:, TPB:TILES, :], x_v[:, TPB:TILES, :]).then_inc(xr_in, 16)
            sp.dma_start(cs[:, TPB:TILES, :], c_v[:, TPB:TILES, :]).then_inc(cr_in, 16)
            sp.dma_start(gwr[:, :], gate_w).then_inc(small_in, 16)
            sp.dma_start(brow[0:RCH, :], be1.rearrange("(c e) i -> c (e i)", e=EPC)).then_inc(small_in, 16)
            sp.dma_start(brow[RCH:CH, :], bs1.rearrange("(a n) -> a n", a=1)).then_inc(small_in, 16)
            sp.dma_start(brow[CH:CH + RCH, :], be3.rearrange("(c e) i -> c (e i)", e=EPC)).then_inc(small_in, 16)
            sp.dma_start(brow[CH + RCH:2 * CH, :], bs3.rearrange("(a n) -> a n", a=1)).then_inc(small_in, 16)
            sp.dma_start(brow[2 * CH:NB1, :], bs2.rearrange("(a n) -> a n", a=1)).then_inc(small_in, 16)
            for part in range(3):
                sp.dma_start(be2f[part * E:(part + 1) * E, :], be2).then_inc(small_in, 16)
            sp.dma_start(spreadf[:, :], spread_in).then_inc(small_in, 16)
            sp.dma_start(w13[:, 0, 0:RCH, :].rearrange("p c (e i) -> p (c e) i", e=EPC),
                         We1.rearrange("e d i -> d e i")).then_inc(w13_in, 16)
            sp.dma_start(w13[:, 1, 0:RCH, :].rearrange("p c (e i) -> p (c e) i", e=EPC),
                         We3.rearrange("e d i -> d e i")).then_inc(w13_in, 16)
            sp.dma_start(w13[:, 0, RCH, :], ws1).then_inc(w13_in, 16)
            sp.dma_start(w13[:, 1, RCH, :], ws3).then_inc(w13_in, 16)
            sp.dma_start(w2[:, 0:RCH, :], We2.rearrange("(c e) i d -> (e i) c d", e=EPC)).then_inc(w2_in, 16)
            sp.dma_start(w2[:, RCH, :], ws2).then_inc(w2_in, 16)
            with sp.Fori(0, B) as b:
                sp.wait_ge(out_ready, b + 1)
                sp.dma_start(out_v[b], outb[:, :, :]).then_inc(out_sent, 16)
            sp.wait_ge(out_sent, 16 * B)

        @block.gpsimd
        def _(pool):
            g = nc.gpsimd

            def parts(b, half, src, rest, cat, places, step, built):
                high, middle, low = places
                v = src[:, half, :, :].rearrange("p n (h d) -> p (n h) d", d=DH)
                rows = cat[:, half, :, :, :].rearrange("p n h r -> p (n h) r")[:, :, 0:QK].rearrange(
                    "p h (c d) -> p h c d", d=DH)

                def at(first, stride, copies):
                    return rows[:, :, first:first + stride * (copies - 1) + 1:stride, :]

                def copy(where, value):
                    return g.tensor_scalar(at(*where), value.unsqueeze(2).to_broadcast(
                        [P, TPB * HPH, where[2], DH]), 1.0, 1.0, ALU.mult, ALU.mult)

                n = 3 * (HALVES * b + half)
                copy(high, v).then_inc(step, 1)
                pool.wait_ge(step, n + 1)
                g.tensor_tensor(rest[:, :, :], v, rows[:, :, high[0], :], ALU.subtract).then_inc(step, 1)
                pool.wait_ge(step, n + 2).then_inc(pool_passed, 1)
                copy(middle, rest[:, :, :]).then_inc(step, 1)
                pool.wait_ge(step, n + 3)
                g.tensor_tensor(rows[:, :, low, :], rest[:, :, :], rows[:, :, middle[0], :],
                                ALU.subtract).then_inc(built, 1)

            def build_q(b, half):
                if not isinstance(b, int) or b > 0:
                    pool.wait_ge(t2_done, UPB * (b - 1) + 2 * half + 2).then_inc(pool_passed, 1)
                pool.wait_ge(qhat_ready, b + 1).then_inc(pool_passed, 1)
                parts(b, half, qhat, qrest, qcat, ((0, 1, 3), (3, 1, 2), 5), q_step, q_built)

            def build_k(b, half):
                if not isinstance(b, int) or b > 0:
                    pool.wait_ge(t_done, UPB * (b - 1) + 2 * half + 2).then_inc(pool_passed, 1)
                pool.wait_ge(kin_ready, b + 1).then_inc(pool_passed, 1)
                parts(b, half, kin, krest, kcat, ((1, 2, 3), (2, 2, 2), 0), k_step, k_built)

            def power(b):
                pool.wait_ge(var_ready, b + 1)
                wait(pool, qhat_ready, b)
                g.tensor_tensor(rstd[:, :], var8[:, :], minus_half[:, 0:TPB], ALU.pow).then_inc(rstd_ready, 1)

            pool.wait_ge(half_set, 1)
            build_k(0, 0)
            power(0)
            build_q(0, 0)
            build_k(0, 1)

            def low_weights(m):
                pool.wait_ge(w_hi, m + 1)
                g.tensor_tensor(w13l[:, m, :, :], w13[:, m, :, :], w13h[:, m, :, :].bitcast(F32),
                                ALU.subtract).then_inc(w_ready, 1)

            def low_biases():
                low = slice(2 * E, 3 * E)
                pool.wait_ge(be2_hi, 1)
                pool.wait_ge(w_ready, 2)
                g.tensor_tensor(be2r[low, :], be2f[low, :], be2r[low, :].bitcast(F32),
                                ALU.subtract).then_inc(be2_ready, 1)
                pool.wait_ge(be2_ready, 1)

            def power2(group):
                part = slice(TPB * STAT_GROUPS[group][0], TPB * STAT_GROUPS[group][1])
                pool.wait_ge(var2_ready, group + 1)
                g.tensor_tensor(rstd2[:, part], var2[:, part], minus_half[:, part], ALU.pow).then_inc(rstd2_ready, 1)

            def normalise(group):
                pool.wait_ge(rstd2_ready, group + 1)
                shape = [P, TPB, D]
                for b in range(*STAT_GROUPS[group]):
                    part = slice(TPB * b, TPB * (b + 1))
                    g.tensor_tensor(centred[:, :, :], xs[:, part, :], mv2[:, part, 0].unsqueeze(2).to_broadcast(shape),
                                    ALU.subtract).then_inc(centred_done, 1)
                    pool.wait_ge(centred_done, b + 1)
                    g.tensor_tensor(xh[:, part, :], centred[:, :, :], rstd2[:, part].unsqueeze(2).to_broadcast(shape),
                                    ALU.mult).then_inc(xh_ready, 1)
                    pool.wait_ge(xh_ready, b + 1)

            def body(b):
                for j in range(UPB):
                    if j == 0 and exists(b):
                        build_q(b, 1)
                        if exists(b + 1):
                            power(b + 1)
                    if j == 1 and exists(b + 1):
                        build_k(b + 1, 0)
                    if j == 2 and exists(b + 1):
                        build_q(b + 1, 0)
                    if j == 3 and exists(b + 1):
                        build_k(b + 1, 1)

            batches(pool, body)

            for group in range(len(STAT_GROUPS) - 1):
                power2(group)
                normalise(group)
                if group in (0, 2):
                    low_weights(group // 2)
            low_biases()
            power2(len(STAT_GROUPS) - 1)

            def experts(b):
                for k in range(RCH):
                    if not exists(b):
                        continue
                    slot = k % SLOTS
                    pool.wait_ge(u_done, CH * b + k + 1)
                    pool.wait_ge(spread_out, RCH * b + k + 1)
                    wait(pool, w2_done, CH * b + k - SLOTS + 1)
                    g.tensor_tensor(hid[:, slot, :], u[:, slot, :], spreadc[:, slot, :], ALU.mult).then_inc(hid_done, 1)

            batches(pool, experts)

        @block.vector
        def _(dve):
            v = nc.vector
            v.memset(warm[:, :], 0.0).then_inc(warm_set, 1)
            v.memset(minus_half[:, :], -0.5).then_inc(half_set, 1)
            v.memset(ones[:, :], 1.0).then_inc(ones_set, 1)

            def tiles(b):
                return bass.ds(TPB * b, TPB)

            def make_kin(b):
                if isinstance(b, int) and b == 0:
                    dve.wait_ge(c0_in, 16)
                if isinstance(b, int) and b == 1:
                    dve.wait_ge(cr_in, 16)
                if not isinstance(b, int) or b > 0:
                    dve.wait_ge(k_built, HALVES * b).then_inc(dve_passed, 1)
                v.tensor_copy(kin[:, :, :, :], cs[:, tiles(b), :].rearrange(
                    "p n (f e) -> p f n e", f=HALVES)).then_inc(kin_ready, 1)

            def tile_stats(b, n):
                if isinstance(b, int) and b == 0 and n == 0:
                    dve.wait_ge(x0_in, 16)
                if isinstance(b, int) and b == 1 and n == 0:
                    dve.wait_ge(xr_in, 16)
                v.bn_stats(stats[:, n, :], xs[:, bass.ds(TPB * b + n, 1), :]).then_inc(stat_done, 1)

            def merge_stats(b):
                dve.wait_ge(stat_done, TPB * (b + 1)).then_inc(dve_passed, 1)
                for n in range(TPB):
                    last = v.bn_aggr(mv[:, n, :], stats[:, n, :])
                last.then_inc(aggr_done, 1)

            def variance(b):
                dve.wait_ge(aggr_done, b + 1)
                wait(dve, rstd_ready, b)
                v.tensor_scalar(var8[:, :], mv[:, :, 1], EPS, float(DH), ALU.add, ALU.mult).then_inc(var_ready, 1)

            def make_qhat(b):
                dve.wait_ge(rstd_ready, b + 1)
                wait(dve, q_built, HALVES * b)
                for n in range(TPB):
                    last = v.tensor_scalar(qhat[:, :, n, :], xs[:, bass.ds(TPB * b + n, 1), :].rearrange(
                        "p n (f e) -> p (n f) e", f=HALVES), mv[:, n, 0:1], rstd[:, n:n + 1], ALU.subtract, ALU.mult)
                last.then_inc(qhat_ready, 1)

            def make_v(b, half):
                if not isinstance(b, int) or b > 0:
                    dve.wait_ge(av_done, UPB * (b - 1) + 2 * half + 2).then_inc(dve_passed, 1)
                src = cs[:, tiles(b), :].rearrange("p n (f h d) -> p n f h d", f=HALVES, d=DH)
                v.tensor_copy(vcat[:, half, :, :, 0:DH], src[:, :, half, :, :]).then_inc(v_ready, 1)

            def second_q(b, j):
                n = UPB * b + j
                dve.wait_ge(t2_done, n + 1)
                wait(dve, st_done, 2 * n - 2)
                v.tensor_copy(q2T[:, j % 2, :, :], ps_t2).then_inc(q2_ready, 1)

            def maximum(b, j, a):
                dve.wait_ge(s_done, 2 * (UPB * b + j) + a + 1)
                v.tensor_reduce(negmax[:, j % 2, 0, 2 * a:2 * a + 2], bank_s[:, :, 0:P], AX_X, ALU.max, negate=True)
                v.tensor_reduce(negmax[:, j % 2, 1, 2 * a:2 * a + 2], bank_s[:, :, P:3 * P], AX_X, ALU.max,
                                negate=True).then_inc(max_done, 1)

            def shift_rows(j):
                half, first = j // 2, (j % 2) * HPU
                return [qcat[:, half, :, first:first + HPU, R_MAX + part] for part in range(2)]

            def tile_stats_2(group):
                first, last_b = STAT_GROUPS[group]
                dve.wait_ge(x1_ready, UPB * last_b)
                for t in range(TPB * first, TPB * last_b):
                    last = v.bn_stats(stats2[:, t, :], xs[:, t, :])
                last.then_inc(stat2_done, 1)

            def merge_stats_2(group):
                first, last_b = STAT_GROUPS[group]
                dve.wait_ge(stat2_done, group + 1)
                for t in range(TPB * first, TPB * last_b):
                    last = v.bn_aggr(mv2[:, t, :], stats2[:, t, :])
                last.then_inc(aggr2_done, 1)

            def variance_2(group):
                part = slice(TPB * STAT_GROUPS[group][0], TPB * STAT_GROUPS[group][1])
                dve.wait_ge(aggr2_done, group + 1)
                v.tensor_scalar(var2[:, part], mv2[:, part, 1], EPS, None, ALU.add).then_inc(var2_ready, 1)

            def stats_2(group):
                tile_stats_2(group)
                merge_stats_2(group)
                variance_2(group)

            def normalise_last():
                dve.wait_ge(rstd2_ready, len(STAT_GROUPS))
                dve.wait_ge(xh_ready, B - 1)
                for t in range(TPB * (B - 1), TILES):
                    last = v.tensor_scalar(xh[:, t, :], xs[:, t, :], mv2[:, t, 0:1], rstd2[:, t:t + 1],
                                           ALU.subtract, ALU.mult)
                last.then_inc(xh_ready, 1)

            def low(group):
                dve.wait_ge(xth_ready, group + 1)
                at, here = routed(group)
                v.tensor_tensor(xTl[:, at], ps_xt[group % 2][:, here], xTh[:, at].bitcast(F32),
                                ALU.subtract).then_inc(xtl_ready, 1)

            shifted, e_val, p_val, biased = (wide[:, n, :, :] for n in range(4))
            shift, total, inv = (one[:, n, :] for n in range(3))

            def softmax_start(part, past):
                first, last = SHARES[part]
                n, m = slice(TPB * first, TPB * last), TPB * (last - first)
                dve.wait_ge(logit_done, [group for group, to in enumerate(ROUTED) if to[0] < last][-1] + 1)
                v.tensor_reduce(shift[:, n], ps_logit[:, n, :], AX_X, ALU.max, negate=True).then_inc(soft_step, 1)
                dve.wait_ge(soft_step, past + 1)
                v.tensor_tensor(shifted[:, n, :], ps_logit[:, n, :], shift[:, n].unsqueeze(2).to_broadcast([P, m, E]),
                                ALU.add).then_inc(logit_ready, 1)

            def softmax_end(first, last, exponentials, past):
                n, m = slice(TPB * first, TPB * last), TPB * (last - first)
                dve.wait_ge(e_ready, exponentials)
                v.tensor_reduce(total[:, n], e_val[:, n, :], AX_X, ALU.add).then_inc(soft_step, 1)
                dve.wait_ge(soft_step, past + 1)
                v.reciprocal(inv[:, n], total[:, n]).then_inc(soft_step, 1)
                dve.wait_ge(soft_step, past + 2)
                v.tensor_tensor(p_val[:, n, :], e_val[:, n, :], inv[:, n].unsqueeze(2).to_broadcast([P, m, E]),
                                ALU.mult).then_inc(soft_step, 1)

            def add_bias(first, last, steps):
                n, m = slice(TPB * first, TPB * last), TPB * (last - first)
                dve.wait_ge(soft_step, steps)
                v.tensor_tensor(biased[:, n, :], p_val[:, n, :], gateb[:, :].unsqueeze(1).to_broadcast([P, m, E]),
                                ALU.add).then_inc(soft_done, 1)

            limited, numbered, hot1, weight1, weight2, weight = (choice[:, n, :, :] for n in range(6))
            per_e, per_g = [P, TPB, E], [P, TPB, GROUPS, GROUPS]
            numbers = cst[:, C_E:C_E + E].unsqueeze(1)
            lower = cst[:, C_LOWER:C_LOWER + GROUPS * GROUPS].rearrange("p (g o) -> p g o", o=GROUPS).unsqueeze(
                1).to_broadcast(per_g)

            def choose(b, part):
                past = CHOOSE_STEPS * b
                quads = biased[:, tiles(b), :].rearrange("p n (g c) -> p (n g) c", c=E // GROUPS)
                hi2, lo2 = minmax[:, 0, :, :], minmax[:, 1, :, :]
                top1, mid1, mid2, top2, score, ahead_of = (narrow[:, n, :] for n in range(6))

                if part == 0:
                    v.tensor_tensor(hi2, quads[:, :, 0:2], quads[:, :, 2:4], ALU.max)
                    v.tensor_tensor(lo2, quads[:, :, 0:2], quads[:, :, 2:4], ALU.min).then_inc(choose_step, 1)
                    dve.wait_ge(choose_step, past + 1)
                    v.tensor_tensor(top1, hi2[:, :, 0], hi2[:, :, 1], ALU.max)
                    v.tensor_tensor(mid1, hi2[:, :, 0], hi2[:, :, 1], ALU.min)
                    v.tensor_tensor(mid2, lo2[:, :, 0], lo2[:, :, 1], ALU.max).then_inc(choose_step, 1)
                    dve.wait_ge(choose_step, past + 2)
                    v.tensor_tensor(top2, mid1, mid2, ALU.max).then_inc(choose_step, 1)
                if part == 1:
                    dve.wait_ge(choose_step, past + 3)
                    v.tensor_tensor(score, top1, top2, ALU.add).then_inc(choose_step, 1)
                    gs = score.rearrange("p (n g) -> p n g", g=GROUPS)
                    other, own = gs.unsqueeze(2).to_broadcast(per_g), gs.unsqueeze(3).to_broadcast(per_g)
                    four = dict(g=GROUPS)
                    dve.wait_ge(choose_step, past + 4)
                    v.tensor_tensor(rank[:, :, 0, :].rearrange("p (n g) o -> p n g o", **four), other, own, ALU.is_gt)
                    v.tensor_tensor(equal[:, :, :].rearrange("p (n g) o -> p n g o", **four), other, own,
                                    ALU.is_equal).then_inc(choose_step, 1)
                    dve.wait_ge(choose_step, past + 5)
                    v.tensor_tensor(rank[:, :, 1, :].rearrange("p (n g) o -> p n g o", **four), equal[:, :, :].rearrange(
                        "p (n g) o -> p n g o", **four), lower, ALU.mult).then_inc(choose_step, 1)
                if part == 2:
                    dve.wait_ge(choose_step, past + 6)
                    v.tensor_reduce(ahead_of, rank[:, :, :, :].rearrange("p m c o -> p m (c o)"), AX_X,
                                    ALU.add).then_inc(choose_step, 1)
                    dve.wait_ge(choose_step, past + 7)
                    v.scalar_tensor_tensor(limited.rearrange("p n (g c) -> p (n g) c", g=GROUPS), ahead_of.unsqueeze(
                        2).to_broadcast([P, TPB * GROUPS, E // GROUPS]), MASKED, quads, ALU.mult,
                        ALU.min).then_inc(choose_step, 1)
                    dve.wait_ge(choose_step, past + 8)
                    v.tensor_reduce(best[:, :], limited, AX_X, ALU.max).then_inc(choose_step, 1)
                if part == 3:
                    dve.wait_ge(choose_step, past + 9)
                    for n in range(TPB):
                        last = v.scalar_tensor_tensor(numbered[:, n:n + 1, :], limited[:, n:n + 1, :],
                                                      best[:, n:n + 1], numbers, ALU.is_equal, ALU.mult)
                    last.then_inc(choose_step, 1)
                    dve.wait_ge(choose_step, past + 10)
                    v.tensor_reduce(first_of[:, :], numbered, AX_X, ALU.max).then_inc(choose_step, 1)
                    dve.wait_ge(choose_step, past + 11)
                    v.tensor_tensor(hot1, first_of[:, :].unsqueeze(2).to_broadcast(per_e), numbers.to_broadcast(per_e),
                                    ALU.is_equal).then_inc(choose_step, 1)
                if part == 4:
                    dve.wait_ge(choose_step, past + 12)
                    v.tensor_tensor(weight1, hot1, p_val[:, tiles(b), :], ALU.mult)
                    v.scalar_tensor_tensor(limited, hot1, MASKED, limited, ALU.mult, ALU.add).then_inc(choose_step, 1)
                if part == 5:
                    dve.wait_ge(choose_step, past + 13)
                    v.tensor_reduce(best[:, :], limited, AX_X, ALU.max).then_inc(choose_step, 1)
                    dve.wait_ge(choose_step, past + 14)
                    for n in range(TPB):
                        last = v.scalar_tensor_tensor(numbered[:, n:n + 1, :], limited[:, n:n + 1, :],
                                                      best[:, n:n + 1], numbers, ALU.is_equal, ALU.mult)
                    last.then_inc(choose_step, 1)
                    dve.wait_ge(choose_step, past + 15)
                    v.tensor_reduce(first_of[:, :], numbered, AX_X, ALU.max).then_inc(choose_step, 1)
                if part == 6:
                    dve.wait_ge(choose_step, past + 16)
                    for n in range(TPB):
                        last = v.scalar_tensor_tensor(weight2[:, n:n + 1, :], numbers, first_of[:, n:n + 1],
                                                      p_val[:, bass.ds(TPB * b + n, 1), :], ALU.is_equal, ALU.mult)
                    last.then_inc(choose_step, 1)
                    dve.wait_ge(choose_step, past + 17)
                    v.tensor_tensor(weight, weight1, weight2, ALU.add).then_inc(choose_step, 1)
                    dve.wait_ge(choose_step, past + 18)
                    wait(dve, ct_done, b)
                    v.tensor_copy(ccat[:, :, 0:3:2, :], weight.unsqueeze(2).to_broadcast(
                        [P, TPB, 2, E])).then_inc(choose_step, 1)
                    dve.wait_ge(choose_step, past + 19)
                    v.tensor_tensor(ccat[:, :, 1, :], weight, ccat[:, :, 0, :].bitcast(F32),
                                    ALU.subtract).then_inc(cc_ready, 1)

            def body(b):
                for j in range(UPB):
                    pb, pj = back(b, j, 1, UPB)
                    ob, oj = back(b, j, 4, UPB)
                    on = UPB * ob + oj
                    o = bank_ot[:, 0, 0:SEQ].rearrange("p (n h w) -> p n h w", n=TPB, w=QUAD)
                    if exists(b):
                        maximum(b, j, 0)
                    if j == 1 and exists(b + 1):
                        variance(b + 1)
                    if exists(pb):
                        second_q(pb, pj)
                    if j == 0 and exists(b + 1):
                        make_kin(b + 1)
                        tile_stats(b + 1, 0)
                    if isinstance(b, int) and b == B - 1:
                        tile_stats_2(j)
                    if j == 2 and exists(b + 1):
                        make_qhat(b + 1)
                    if j == 3 and exists(b):
                        for half in range(HALVES):
                            make_v(b, half)
                    if exists(b):
                        maximum(b, j, 1)
                        row_hi, row_lo = shift_rows(j)
                        dve.wait_ge(max_done, 2 * (UPB * b + j) + 2)
                        v.tensor_copy(row_hi, negmax[:, j % 2, :, :]).then_inc(chi_done, 1)
                    if isinstance(b, int) and b == B:
                        if j == 2:
                            softmax_end(0, 1, 1, 1)
                            add_bias(0, 1, 4)
                    if exists(ob):
                        dve.wait_ge(ot_done, on + 1)
                        v.reciprocal(rsum[:, :, :], o[:, :, :, DH]).then_inc(recip_done, 1)
                    if exists(b):
                        dve.wait_ge(chi_done, UPB * b + j + 1)
                        v.tensor_tensor(row_lo, negmax[:, j % 2, :, :], row_hi, ALU.subtract).then_inc(c_ready, 1)
                    if exists(ob):
                        dve.wait_ge(recip_done, on + 1)
                        v.tensor_tensor(onorm[:, :, :].rearrange("p n (h d) -> p n h d", d=DH), o[:, :, :, 0:DH],
                                        rsum[:, :, :].unsqueeze(3).to_broadcast([P, TPB, HPU, DH]),
                                        ALU.mult).then_inc(o_read, 1)
                    if j == 0 and exists(b + 1):
                        tile_stats(b + 1, 1)
                    if isinstance(b, int) and b == B - 1:
                        merge_stats_2(j)
                    if exists(ob):
                        dve.wait_ge(o_read, on + 1)
                        columns = slice(oj * HPU * DH, (oj + 1) * HPU * DH)
                        v.scalar_tensor_tensor(xs[:, tiles(ob), columns], onorm[:, :, :], tg[:, 0:1],
                                               xs[:, tiles(ob), columns], ALU.mult, ALU.add).then_inc(x1_ready, 1)
                    if j == 0 and exists(b + 1):
                        merge_stats(b + 1)
                    if isinstance(b, int) and b == B - 1:
                        variance_2(j)
                    if isinstance(b, int) and b == B:
                        if j == 0:
                            dve.wait_ge(gw_hi, 1)
                            v.tensor_tensor(gwT[:, 1, :], ps_w[:, 0:E], gwT[:, 0, :].bitcast(F32),
                                            ALU.subtract).then_inc(gw_ready, 1)
                        if j < 3:
                            low(j)
                        if j < 2:
                            stats_2(4 + j)
                        if j == 2:
                            dve.wait_ge(soft_done, 1)
                            choose(0, 0)
                        if j == 1:
                            softmax_start(0, 0)
                        if j == 3:
                            stats_2(6)
                            low(3)
                            choose(0, 1)
                            normalise_last()
                            choose(0, 2)
                            low(4)
                            softmax_start(1, 4)
                            choose(0, 3)
                            choose(0, 4)
                            softmax_start(2, 5)
                            choose(0, 5)

            for n in range(TPB):
                tile_stats(0, n)
            merge_stats(0)
            variance(0)
            make_kin(0)
            qrows = qcat[:, :, :, :, :].rearrange("p f n h r -> p (f n h) r")
            krows = kcat[:, :, :, :, :].rearrange("p f n h r -> p (f n h) r")
            v.memset(qrows[:, :, R_MAX:ROWS], 0.0)
            v.memset(krows[:, :, R_MAX:K_ST], 1.0)
            v.memset(krows[:, :, K_ST:ROWS], 0.0)
            dve.wait_ge(cst_in, 16)
            for half in range(HALVES):
                slopes = cst[:, C_SLOPE + half * 3 * HPH:C_SLOPE + (half + 1) * 3 * HPH].rearrange(
                    "p (h c) -> p h c", c=3)
                for n in range(TPB):
                    v.tensor_copy(qcat[:, half, n, :, R_SLOPE:R_MAX], slopes)
            for n in range(TPB):
                last = v.tensor_copy(kcat[:, :, n, :, R_SLOPE:R_MAX],
                                     cst[:, C_POS + n:C_POS + n + 1].unsqueeze(2).unsqueeze(3).to_broadcast(
                                         [P, HALVES, HPH, 3]))
            v.tensor_copy(identb[:, :], ident)
            v.tensor_copy(maskb[:, :], cst[:, C_MASK:C_MASK + P]).then_inc(consts_set, 1)
            make_qhat(0)
            v.memset(vcat[:, :, :, :, :], 0.0).then_inc(values_clear, 1)
            dve.wait_ge(values_clear, 1)
            v.memset(vcat[:, :, :, :, DH].rearrange("p f n h -> p (f n) h"), 1.0)
            dve.wait_ge(tg_ready, 1)
            batches(dve, body)

            choose(0, 6)
            softmax_end(1, B, 3, 6)

            dve.wait_ge(small_ready, 1)
            def experts(b):
                for k in range(CH):
                    pb = b - 1
                    if k == 4 and exists(pb):
                        dve.wait_ge(yt_done, pb + 1)
                        v.scalar_tensor_tensor(outb[:, :, :], ps_yt.rearrange("p (n d) -> p n d", n=TPB), tg[:, 1:2],
                                               xs[:, tiles(pb), :], ALU.mult, ALU.add).then_inc(out_ready, 1)
                    if not exists(b):
                        continue
                    if k == RCH and exists(pb):
                        dve.wait_ge(out_sent, 16 * (pb + 1))
                    c = CH * b + k
                    dve.wait_ge(silu_done, c + 1)
                    ub, uk = back(b, k, SLOTS, CH)
                    wait(dve, hid_done, RCH * ub + min(uk + 1, RCH))
                    target = u
                    if k == RCH:
                        target = hid
                        wait(dve, w2_done, c - SLOTS + 1)
                    v.scalar_tensor_tensor(target[:, k % SLOTS, :], ps_h[k % SLOTS][:, SEQ:2 * SEQ],
                                           bcol[:, CH + k:CH + k + 1], s1[:, k % SLOTS, :],
                                           ALU.add, ALU.mult).then_inc(u_done, 1)
                    if isinstance(b, int) and b == 0 and k == 0:
                        add_bias(1, B, 9)
                        dve.wait_ge(soft_done, 2)
                    if exists(b + 1) and k < CHOOSE_PARTS:
                        choose(b + 1, k)

            batches(dve, experts)

        @block.scalar
        def _(act):
            s = nc.scalar
            act.dma_start(cst[:, :], const_in).then_inc(cst_in, 16)
            act.dma_start(gl[:, 0:1], g_xattn.rearrange("(a n) -> a n", a=1)).then_inc(gl_in, 16)
            act.dma_start(gl[:, 1:2], g_ffn.rearrange("(a n) -> a n", a=1)).then_inc(gl_in, 16)
            act.dma_start(gl[:, 2:2 + E], gate_b.rearrange("(a n) -> a n", a=1)).then_inc(gl_in, 16)
            act.wait_ge(gl_done, 1)
            s.activation(tg[:, :], bank_ot[:, 0, 0:2], ACT.Tanh)
            s.copy(gateb[:, :], bank_ot[:, 0, 2:2 + E]).then_inc(tg_ready, 1)

            def operands(b, j):
                n = UPB * b + j
                act.wait_ge(t_done, n + 1)
                wait(act, st_done, 2 * (n - UPB) + 2)
                s.copy(qkT[:, j, :, :], ps_t).then_inc(qk_ready, 1)

            def exponent(b, j, a):
                n = UPB * b + j
                act.wait_ge(st_done, 2 * n + a + 1)
                wait(act, av_done, n - 1)
                s.activation(prob[:, j % 2, 2 * a:2 * a + 2, :], bank_st[:, :, 0:3 * P], ACT.Exp).then_inc(exp_done, 1)

            def outputs(b, j):
                n = UPB * b + j
                act.wait_ge(av_done, n + 1)
                wait(act, ot_done, n - 1)
                s.copy(avT[:, j % 2, :], bank_av[:, 0, 0:SEQ]).then_inc(av_out, 1)

            def high(group):
                act.wait_ge(xt_done, group + 1)
                at, here = routed(group)
                s.copy(xTh[:, at], ps_xt[group % 2][:, here]).then_inc(xth_ready, 1)

            def log_out(group):
                act.wait_ge(logT_done, group + 1)
                wait(act, logit_done, group - 1)
                _, here = routed(group)
                s.copy(logT[:, group % 2, here], ps_logT[:, here]).then_inc(logT_out, 1)

            def softmax_exp(part):
                act.wait_ge(logit_ready, part + 1)
                n = slice(TPB * SHARES[part][0], TPB * SHARES[part][1])
                s.activation(wide[:, 1, n, :], wide[:, 0, n, :], ACT.Exp).then_inc(e_ready, 1)

            operands(0, 0)

            def body(b):
                for j in range(UPB):
                    nb, nj = back(b, j, -1, UPB)
                    eb, ej = back(b, j, 2, UPB)
                    ab, aj = back(b, j, 3, UPB)
                    if exists(eb):
                        exponent(eb, ej, 0)
                    if isinstance(b, int) and b == B:
                        if j == 2:
                            softmax_exp(0)
                        if j > 0:
                            log_out(j - 1)
                        if j == 0:
                            act.wait_ge(wt_done, 1)
                            s.copy(bcol[:, :], ps_w[:, E:E + NB1])
                            s.copy(gwT[:, 0, :], ps_w[:, 0:E]).then_inc(gw_hi, 1)
                        high(j)
                    if exists(b) and exists(nb):
                        operands(nb, nj)
                    if exists(eb):
                        exponent(eb, ej, 1)
                    if exists(ab):
                        outputs(ab, aj)
                    if isinstance(b, int) and b == B - 1:
                        if j == 0:
                            act.wait_ge(w13_in, 16 * 4)
                            s.copy(w13h[:, 0, :, :], w13[:, 0, :, :]).then_inc(w_hi, 1)
                        if j == 1:
                            s.copy(w13h[:, 1, :, :], w13[:, 1, :, :]).then_inc(w_hi, 1)
                        if j == 2:
                            act.wait_ge(small_in, 16 * 10)
                            s.copy(be2r[:, :], be2f[:, :]).then_inc(be2_hi, 1)
                            s.copy(spreadr[:, :], spreadf[:, :]).then_inc(small_ready, 1)

            batches(act, body)

            log_out(3)
            high(4)
            softmax_exp(1)
            log_out(4)
            softmax_exp(2)

            def weights_out(b):
                act.wait_ge(ct_done, b + 1)
                s.copy(cT[:, bass.ds(SEQ * b, SEQ)], ps_ct).then_inc(ct_ready, 1)

            def experts(b):
                for k in range(CH):
                    c, slot = CH * b + k, k % SLOTS
                    if exists(b):
                        act.wait_ge(h_done, c + 1)
                        wait(act, u_done, c - SLOTS + 1)
                        s.activation(s1[:, slot, :], ps_h[slot][:, 0:SEQ], ACT.Silu,
                                     bias=bcol[:, k:k + 1]).then_inc(silu_done, 1)
                    if isinstance(b, int) and b == 0 and k == 0:
                        weights_out(0)
                    if k == 1 and exists(b - 1):
                        act.wait_ge(w2_done, CH * b)
                        s.activation(yT[:, :], ps_y, ACT.Identity, bias=bcol[:, 2 * CH:NB1]).then_inc(y_out, 1)
                    if not exists(b):
                        continue
                    if k < RCH:
                        cb, ck = back(b, k, SLOTS, CH)
                        act.wait_ge(c_done, RCH * b + k + 1)
                        wait(act, hid_done, RCH * cb + min(ck + 1, RCH))
                        s.copy(spreadc[:, slot, :], ps_c[slot][:, 0:SEQ]).then_inc(spread_out, 1)
                    elif exists(b + 1):
                        weights_out(b + 1)

            batches(act, experts)

        @block.tensor
        def _(pe):
            mm, transpose = nc.tensor.matmul, nc.tensor.transpose
            mask = maskb[:, :].unsqueeze(1).to_broadcast([P, 2, P])
            eye = identb[:, :].unsqueeze(1).to_broadcast([P, 2, P])

            def transposed(b, j):
                n, half, first = UPB * b + j, j // 2, (j % 2) * HPU
                pe.wait_ge(q_built, HALVES * b + half + 1)
                pe.wait_ge(k_built, HALVES * b + half + 1)
                wait(pe, qk_ready, n)
                for a in range(2):
                    for which, cat in enumerate((qcat, kcat)):
                        for t in range(TPB):
                            at = (which * TPB + t) * P
                            last = transpose(ps_t[:, a, at:at + P], cat[:, half, t, first + 2 * a:first + 2 * a + 2, :]
                                             .rearrange("p h r -> p (h r)"), identb[:, :])
                last.then_inc(t_done, 1)

            def scores(b, j, a):
                n = UPB * b + j
                pe.wait_ge(qk_ready, n + 1)
                wait(pe, max_done, 2 * n + a)
                for p in range(2):
                    rows = slice(p * ROWS, p * ROWS + K_S)
                    q, k = qkT[rows, j, a, 0:SEQ], qkT[rows, j, a, SEQ:2 * SEQ]
                    diagonal = bank_s[:, p, 0:3 * P].rearrange("p (x n) -> p x n", n=P)[:, 0:3:2, :]
                    mm(diagonal, identb[:, :], mask, start=True, stop=False, skip_group_check=True)
                    mm(bank_s[:, p, 0:P], q[:, 0:P], k[:, 0:P], start=False, stop=True, skip_group_check=True)
                    last = mm(bank_s[:, p, P:3 * P], q[:, P:SEQ], k, start=False, stop=True, skip_group_check=True)
                last.then_inc(s_done, 1)

            def second(b, j):
                n, half, first = UPB * b + j, j // 2, (j % 2) * HPU
                pe.wait_ge(c_ready, n + 1)
                wait(pe, q2_ready, n)
                for a in range(2):
                    for t in range(TPB):
                        last = transpose(ps_t2[:, a, t * P:(t + 1) * P], qcat[:, half, t, first + 2 * a:first + 2 * a + 2, :]
                                         .rearrange("p h r -> p (h r)"), identb[:, :])
                last.then_inc(t2_done, 1)

            def scores_t(b, j, a):
                n = UPB * b + j
                pe.wait_ge(q2_ready, n + 1)
                wait(pe, exp_done, 2 * n + a)
                for p in range(2):
                    rows = slice(p * ROWS, p * ROWS + K_ST)
                    k = qkT[rows, j, a, SEQ:2 * SEQ]
                    diagonal = bank_st[:, p, 0:3 * P].rearrange("p (x n) -> p x n", n=P)[:, 0:3:2, :]
                    mm(diagonal, maskb[:, :], eye, start=True, stop=False, skip_group_check=True)
                    mm(bank_st[:, p, 0:SEQ], k[:, 0:P], q2T[rows, j % 2, a, :], start=False, stop=True, skip_group_check=True)
                    last = mm(bank_st[:, p, SEQ:3 * P], k[:, P:SEQ], q2T[rows, j % 2, a, P:SEQ], start=False, stop=True,
                              skip_group_check=True)
                last.then_inc(st_done, 1)

            def values(b, j):
                n, half, first = UPB * b + j, j // 2, (j % 2) * HPU
                pe.wait_ge(exp_done, 2 * n + 2)
                pe.wait_ge(v_ready, HALVES * b + half + 1)
                wait(pe, av_out, n)
                for h in range(HPU):
                    mm(bank_av[h * QUAD:(h + 1) * QUAD, 0, 0:SEQ], vcat[:, half, 0, first + h, :],
                       prob[:, j % 2, h, 0:SEQ], start=True, stop=False, skip_group_check=True,
                       tile_position=(0, h * QUAD))
                for h in range(HPU):
                    last = mm(bank_av[h * QUAD:(h + 1) * QUAD, 0, P:SEQ], vcat[:, half, 1, first + h, :],
                              prob[:, j % 2, h, SEQ:3 * P], start=False, stop=True, skip_group_check=True,
                              tile_position=(0, h * QUAD))
                last.then_inc(av_done, 1)

            def outputs(b, j):
                n = UPB * b + j
                pe.wait_ge(av_out, n + 1)
                wait(pe, o_read, n)
                for t in range(TPB):
                    last = transpose(bank_ot[:, 0, t * P:(t + 1) * P], avT[:, j % 2, t * P:(t + 1) * P], ident)
                last.then_inc(ot_done, 1)

            def small_transposes():
                pe.wait_ge(small_in, 16 * 10)
                pe.wait_ge(max_done, 2 * UNITS)
                transpose(ps_w[:, 0:E], gwr[:, :], ident[0:E, 0:E])
                transpose(ps_w[:, E:E + NB1], brow[:, :], ident[0:NB1, 0:NB1]).then_inc(wt_done, 1)

            def tokens_t(b):
                group = [n for n, (first, last) in enumerate(ROUTED) if first <= b < last][0]
                pe.wait_ge(xh_ready, b + 1)
                wait(pe, xtl_ready, group - 1)
                if group == 0:
                    pe.wait_ge(qk_ready, UNITS)
                if group == 1:
                    pe.wait_ge(q2_ready, UNITS)
                for n in range(TPB):
                    at = (TPB * (b - ROUTED[group][0]) + n) * P
                    last = transpose(ps_xt[group % 2][:, at:at + P], xh[:, TPB * b + n, :], ident)
                if b + 1 == ROUTED[group][1]:
                    last.then_inc(xt_done, 1)

            def logits(group):
                pe.wait_ge(gw_ready, 1)
                pe.wait_ge(xtl_ready, group + 1)
                wait(pe, logT_out, group)
                at, here = routed(group)
                mm(ps_logT[:, here], gwT[:, 0, :], xTh[:, at], start=True, stop=False)
                mm(ps_logT[:, here], gwT[:, 1, :], xTh[:, at], start=False, stop=False)
                mm(ps_logT[:, here], gwT[:, 0, :], xTl[:, at], start=False, stop=True).then_inc(logT_done, 1)

            def by_token(group):
                pe.wait_ge(logT_out, group + 1)
                if group in (1, 4):
                    pe.wait_ge(logit_ready, 1 + group // 4)
                first, last_b = ROUTED[group]
                for n in range(TPB * (last_b - first)):
                    last = transpose(ps_logit[:, TPB * first + n, :], logT[:, group % 2, n * P:(n + 1) * P],
                                     ident[0:E, 0:E])
                last.then_inc(logit_done, 1)

            def keep_warm(products):
                for _ in range(products):
                    mm(bank_av[:, 0, :], warm[:, 0:P], warm[:, :], start=True, stop=True)

            pe.wait_ge(warm_set, 1)
            keep_warm(WARM_UP)

            pe.wait_ge(ones_set, 1)
            pe.wait_ge(gl_in, 16 * 3)
            mm(bank_ot[:, 0, 0:2 + E], ones[:, :], gl[:, :], start=True, stop=True).then_inc(gl_done, 1)
            pe.wait_ge(consts_set, 1)
            transposed(0, 0)
            keep_warm(4)

            def body(b):
                for j in range(UPB):
                    nb, nj = back(b, j, -1, UPB)
                    pb, pj = back(b, j, 1, UPB)
                    ab, aj = back(b, j, 3, UPB)
                    ob, oj = back(b, j, 4, UPB)
                    eb, ej = back(b, j, 2, UPB)
                    if isinstance(b, int) and b == B and j == 0:
                        small_transposes()
                    if exists(b):
                        scores(b, j, 0)
                    if exists(pb):
                        second(pb, pj)
                    if exists(eb):
                        scores_t(eb, ej, 0)
                    if isinstance(b, int) and b == B and j < 2:
                        if j == 1:
                            logits(0)
                        tokens_t(2 * j)
                        tokens_t(2 * j + 1)
                    if exists(b) and exists(nb):
                        transposed(nb, nj)
                    if isinstance(b, int) and b == 0 and j < 3:
                        keep_warm(3)
                    if exists(ob) and not (isinstance(b, int) and b == B and j == 3):
                        if isinstance(ob, int) and ob == 0:
                            pe.wait_ge(tg_ready, 1)
                        outputs(ob, oj)
                    if exists(b):
                        scores(b, j, 1)
                    if isinstance(b, int) and b == 0 and j < 2:
                        keep_warm(5)
                    if exists(eb):
                        scores_t(eb, ej, 1)
                    if exists(ab):
                        values(ab, aj)
                    if isinstance(b, int) and b == B and j > 0:
                        by_token(j - 1)
                        if j == 2:
                            outputs(B - 1, UPB - 1)
                        if j < 3:
                            logits(j)
                            tokens_t(2 * j + 2)
                        if j < 2:
                            tokens_t(2 * j + 3)

            batches(pe, body)

            keep_warm(4)
            logits(3)
            keep_warm(3)
            tokens_t(B - 1)
            by_token(3)
            keep_warm(2)
            logits(4)
            keep_warm(3)
            by_token(4)

            pe.wait_ge(w_ready, 2)
            pe.wait_ge(be2_ready, 1)
            pe.wait_ge(small_ready, 1)
            pe.wait_ge(w2_in, 16 * 2)

            def weights_t(b):
                pe.wait_ge(cc_ready, b + 1).then_inc(pe_passed, 1)
                for n in range(TPB):
                    last = transpose(ps_ct[:, n * P:(n + 1) * P], ccat[:, n, :, :].rearrange("p c e -> p (c e)").bitcast(F32), ident)
                last.then_inc(ct_done, 1)

            def hidden(b, k):
                slot, tokens = k % SLOTS, bass.ds(SEQ * b, SEQ)
                cb, ck = back(b, k, SLOTS, CH)
                wait(pe, spread_out, RCH * cb + min(ck + 1, RCH))
                wait(pe, u_done, CH * b + k - SLOTS + 1)
                for m in range(2):
                    target = ps_h[slot][:, m * SEQ:(m + 1) * SEQ]
                    mm(target, w13h[:, m, k, :], xTh[:, tokens], start=True, stop=False, skip_group_check=True)
                    mm(target, w13h[:, m, k, :], xTl[:, tokens], start=False, stop=False, skip_group_check=True)
                    last = mm(target, w13l[:, m, k, :], xTh[:, tokens], start=False, stop=True, skip_group_check=True)
                last.then_inc(h_done, 1)

            def spread(b, k):
                slot, tokens = k % SLOTS, bass.ds(SEQ * b, SEQ)
                if k == 0:
                    pe.wait_ge(ct_ready, b + 1).then_inc(pe_passed, 1)
                if k < RCH:
                    mm(ps_c[slot][:, 0:SEQ], spreadr[:, k * P:(k + 1) * P], cT[0:2 * E, tokens],
                       start=True, stop=True).then_inc(c_done, 1)

            def down(b, k):
                if k == 0:
                    wait(pe, y_out, b)
                if k < RCH:
                    pe.wait_ge(hid_done, RCH * b + k + 1)
                else:
                    pe.wait_ge(u_done, CH * b + k + 1)
                last = mm(ps_y, w2[:, k, :], hid[:, k % SLOTS, :], start=k == 0, stop=k == RCH, skip_group_check=True)
                if k == 0:
                    last = mm(ps_y, be2r[:, :], cT[:, bass.ds(SEQ * b, SEQ)], start=False, stop=False,
                              skip_group_check=True)
                last.then_inc(w2_done, 1)

            def experts(b):
                for k in range(CH):
                    if exists(b) and not (isinstance(b, int) and b == 0 and k <= SLOTS):
                        hidden(b, k)
                    if isinstance(b, int) and b == 0 and k == 0:
                        hidden(0, 0)
                        hidden(0, 1)
                        hidden(0, 2)
                        keep_warm(2)
                        weights_t(0)
                        keep_warm(2)
                        pe.wait_ge(logit_ready, 3)
                    if exists(b):
                        spread(b, k)
                    db, dk = back(b, k, 2, CH)
                    if isinstance(b, int) and b == 0 and k == 2:
                        hidden(0, SLOTS)
                        keep_warm(2)
                    if k == 3 and exists(b - 1):
                        pe.wait_ge(y_out, b)
                        for n in range(TPB):
                            last = transpose(ps_yt[:, n * P:(n + 1) * P], yT[:, n * P:(n + 1) * P], ident)
                        last.then_inc(yt_done, 1)
                    if k == CH - 1 and exists(b) and exists(b + 1):
                        weights_t(b + 1)
                    if exists(db):
                        down(db, dk)

            batches(pe, experts)


def kernel(**inputs):
    import numpy as np
    import concourse.bacc as bacc
    from concourse import mybir
    from concourse.bass_utils import run_bass_kernel_spmd
    nc = bacc.Bacc("TRN2", target_bir_lowering=False, num_devices=1)
    table, spread = constants()
    arrays = {"x": np.ascontiguousarray(inputs["x"]).reshape(B * SEQ, D),
              "ctx": np.ascontiguousarray(inputs["ctx_1024"]).reshape(B * SEQ, D),
              "g_xattn": np.ascontiguousarray(inputs["g_xattn"]),
              "g_ffn": np.ascontiguousarray(inputs["g_ffn"])}
    for name in ("gate_w", "gate_b", "We1", "be1", "We2", "be2", "We3", "be3", "ws1", "bs1", "ws2", "bs2", "ws3", "bs3"):
        arrays[name] = np.ascontiguousarray(inputs["L0_ffn_" + name])
    arrays["table"], arrays["spread"] = table, spread
    ins = [nc.dram_tensor(name + "_in", a.shape, mybir.dt.float32, kind="ExternalInput").ap()
           for name, a in arrays.items()]
    out = nc.dram_tensor("y_out", (B * SEQ, D), mybir.dt.float32, kind="ExternalOutput").ap()
    program(nc, *ins, out)
    res = run_bass_kernel_spmd(nc, [{name + "_in": a for name, a in arrays.items()}], core_ids=[0])
    return res.results[0]["y_out"].reshape(B, SEQ, D)
```
